# Optimizing a Trainium2 kernel written in Bass

```python
import numpy as np
import jax
import jax.numpy as jnp

def _softmax(x, axis=-1):
    return jax.nn.softmax(x, axis=axis)

def _gelu(x):
    return jax.nn.gelu(x, approximate=True)

def _silu(x):
    return jax.nn.silu(x)

def _sigmoid(x):
    return jax.nn.sigmoid(x)

def _layernorm(x, axis=-1, eps=1e-05):
    m = jnp.mean(x, axis=axis, keepdims=True)
    v = jnp.var(x, axis=axis, keepdims=True)
    return (x - m) / jnp.sqrt(v + eps)

def _scatter_add(tgt, idx, src, axis=0):
    return tgt.at[idx].add(src)

def _segment_sum(src, seg, n):
    return jax.ops.segment_sum(src, seg, n)
kernel_name = 'mk_sandwich_d1_jaxref_r4_19d24e'

def setup_inputs(seed: int=0):
    np.random.seed(seed)
    _w = jnp.asarray

    def _L0_attn_setup():
        import jax, jax.numpy as jnp
        import numpy as np
        D_MODEL = 256
        D_STATE = 16
        EXPAND = 2
        D_CONV = 4
        D_INNER = D_MODEL * EXPAND
        DT_RANK = 64
        BATCH = 2
        SEQLEN = 512

        def _causal_conv_silu(x, w, b):
            K = w.shape[-1]
            xc = jnp.transpose(x, (0, 2, 1))
            xc = jnp.pad(xc, ((0, 0), (0, 0), (K - 1, 0)))
            y = jax.lax.conv_general_dilated(xc, w, (1,), 'VALID', dimension_numbers=('NCH', 'OIH', 'NCH'), feature_group_count=w.shape[0])
            y = y + b[None, :, None]
            return jax.nn.silu(jnp.transpose(y, (0, 2, 1)))

        def _ssm_scan(x, dt, A, Bm, Cm, D, z):

            def step(h, inp):
                x_t, dt_t, B_t, C_t = inp
                dA = jnp.exp(dt_t[:, :, None] * A[None])
                h = dA * h + (dt_t * x_t)[:, :, None] * B_t[:, None, :]
                y = jnp.einsum('bdn,bn->bd', h, C_t) + D * x_t
                return (h, y)
            Bz, L, Di = x.shape
            h0 = jnp.zeros((Bz, Di, A.shape[1]), x.dtype)
            xs = (x.swapaxes(0, 1), dt.swapaxes(0, 1), Bm.swapaxes(0, 1), Cm.swapaxes(0, 1))
            _, ys = jax.lax.scan(step, h0, xs)
            return ys.swapaxes(0, 1) * jax.nn.silu(z)

        def _branch(x_in, z, conv_w, conv_b, xp_w, dt_w, dt_b, A_log, Dp):
            xc = _causal_conv_silu(x_in, conv_w, conv_b)
            proj = xc @ xp_w.T
            dt, Bm, Cm = jnp.split(proj, [DT_RANK, DT_RANK + D_STATE], axis=-1)
            dt = jax.nn.softplus(dt @ dt_w.T + dt_b)
            return _ssm_scan(xc, dt, -jnp.exp(A_log), Bm, Cm, Dp, z)
        key = jax.random.key(seed)
        ks = jax.random.split(key, 16)
        s = 0.02
        inp = {'u': jax.random.normal(ks[0], (BATCH, SEQLEN, D_MODEL), jnp.float32), 'in_proj_w': jax.random.normal(ks[1], (2 * D_INNER, D_MODEL), jnp.float32) * s, 'out_proj_w': jax.random.normal(ks[2], (D_MODEL, D_INNER), jnp.float32) * s, 'fwd_conv_w': jax.random.normal(ks[3], (D_INNER, 1, D_CONV), jnp.float32) * 0.1, 'fwd_conv_b': jax.random.normal(ks[4], (D_INNER,), jnp.float32) * 0.01, 'fwd_x_proj_w': jax.random.normal(ks[5], (DT_RANK + 2 * D_STATE, D_INNER), jnp.float32) * s, 'fwd_dt_w': jax.random.normal(ks[6], (D_INNER, DT_RANK), jnp.float32) * s, 'fwd_dt_b': jax.random.normal(ks[7], (D_INNER,), jnp.float32) * 0.01, 'fwd_A_log': jnp.tile(jnp.log(jnp.arange(1, D_STATE + 1, dtype=jnp.float32)), (D_INNER, 1)), 'fwd_D': jnp.ones((D_INNER,), jnp.float32), 'bwd_conv_w': jax.random.normal(ks[8], (D_INNER, 1, D_CONV), jnp.float32) * 0.1, 'bwd_conv_b': jax.random.normal(ks[9], (D_INNER,), jnp.float32) * 0.01, 'bwd_x_proj_w': jax.random.normal(ks[10], (DT_RANK + 2 * D_STATE, D_INNER), jnp.float32) * s, 'bwd_dt_w': jax.random.normal(ks[11], (D_INNER, DT_RANK), jnp.float32) * s, 'bwd_dt_b': jax.random.normal(ks[12], (D_INNER,), jnp.float32) * 0.01, 'bwd_A_log': jnp.tile(jnp.log(jnp.arange(1, D_STATE + 1, dtype=jnp.float32)), (D_INNER, 1)), 'bwd_D': jnp.ones((D_INNER,), jnp.float32)}
        return inp
    _L0_attn_in = _L0_attn_setup()

    def _L0_ffn_setup():
        import jax, jax.numpy as jnp
        import numpy as np
        DIM = 256
        HIDDEN = 768
        SCALE = 1.0 / 127.0

        def _dequant(w_int, dtype):
            return w_int.astype(dtype) * jnp.asarray(SCALE, dtype)
        key = jax.random.key(seed)
        k_x, k_g, k_u, k_d = jax.random.split(key, 4)
        x = jax.random.normal(k_x, (4, 512, DIM), dtype=jnp.float32)
        w_gate = jax.random.randint(k_g, (HIDDEN, DIM), -127, 128, dtype=jnp.int32)
        w_up = jax.random.randint(k_u, (HIDDEN, DIM), -127, 128, dtype=jnp.int32)
        w_down = jax.random.randint(k_d, (DIM, HIDDEN), -127, 128, dtype=jnp.int32)
        return {'x': x, 'w_gate': w_gate, 'w_up': w_up, 'w_down': w_down}
    _L0_ffn_in = _L0_ffn_setup()
    _d = {'L0_attn_u': _L0_attn_in['u'], 'L0_attn_in_proj_w': _L0_attn_in['in_proj_w'], 'L0_attn_out_proj_w': _L0_attn_in['out_proj_w'], 'L0_attn_fwd_conv_w': _L0_attn_in['fwd_conv_w'], 'L0_attn_fwd_conv_b': _L0_attn_in['fwd_conv_b'], 'L0_attn_fwd_x_proj_w': _L0_attn_in['fwd_x_proj_w'], 'L0_attn_fwd_dt_w': _L0_attn_in['fwd_dt_w'], 'L0_attn_fwd_dt_b': _L0_attn_in['fwd_dt_b'], 'L0_attn_fwd_A_log': _L0_attn_in['fwd_A_log'], 'L0_attn_fwd_D': _L0_attn_in['fwd_D'], 'L0_attn_bwd_conv_w': _L0_attn_in['bwd_conv_w'], 'L0_attn_bwd_conv_b': _L0_attn_in['bwd_conv_b'], 'L0_attn_bwd_x_proj_w': _L0_attn_in['bwd_x_proj_w'], 'L0_attn_bwd_dt_w': _L0_attn_in['bwd_dt_w'], 'L0_attn_bwd_dt_b': _L0_attn_in['bwd_dt_b'], 'L0_attn_bwd_A_log': _L0_attn_in['bwd_A_log'], 'L0_attn_bwd_D': _L0_attn_in['bwd_D'], 'L0_ffn_w_gate': _L0_ffn_in['w_gate'], 'L0_ffn_w_up': _L0_ffn_in['w_up'], 'L0_ffn_w_down': _L0_ffn_in['w_down']}
    _x0 = _d['L0_attn_u']
    _d['L0_attn_u'] = jax.random.normal(jax.random.fold_in(jax.random.key(seed), 1), (8, 512, 256), dtype=_x0.dtype)
    del _x0
    return _d

def reference(L0_attn_u, L0_attn_in_proj_w, L0_attn_out_proj_w, L0_attn_fwd_conv_w, L0_attn_fwd_conv_b, L0_attn_fwd_x_proj_w, L0_attn_fwd_dt_w, L0_attn_fwd_dt_b, L0_attn_fwd_A_log, L0_attn_fwd_D, L0_attn_bwd_conv_w, L0_attn_bwd_conv_b, L0_attn_bwd_x_proj_w, L0_attn_bwd_dt_w, L0_attn_bwd_dt_b, L0_attn_bwd_A_log, L0_attn_bwd_D, L0_ffn_w_gate, L0_ffn_w_up, L0_ffn_w_down):

    def _L0_attn_ref(u, in_proj_w, out_proj_w, fwd_conv_w, fwd_conv_b, fwd_x_proj_w, fwd_dt_w, fwd_dt_b, fwd_A_log, fwd_D, bwd_conv_w, bwd_conv_b, bwd_x_proj_w, bwd_dt_w, bwd_dt_b, bwd_A_log, bwd_D):
        import jax, jax.numpy as jnp
        import numpy as np
        D_MODEL = 256
        D_STATE = 16
        EXPAND = 2
        D_CONV = 4
        D_INNER = D_MODEL * EXPAND
        DT_RANK = 64
        BATCH = 2
        SEQLEN = 512

        def _causal_conv_silu(x, w, b):
            K = w.shape[-1]
            xc = jnp.transpose(x, (0, 2, 1))
            xc = jnp.pad(xc, ((0, 0), (0, 0), (K - 1, 0)))
            y = jax.lax.conv_general_dilated(xc, w, (1,), 'VALID', dimension_numbers=('NCH', 'OIH', 'NCH'), feature_group_count=w.shape[0])
            y = y + b[None, :, None]
            return jax.nn.silu(jnp.transpose(y, (0, 2, 1)))

        def _ssm_scan(x, dt, A, Bm, Cm, D, z):

            def step(h, inp):
                x_t, dt_t, B_t, C_t = inp
                dA = jnp.exp(dt_t[:, :, None] * A[None])
                h = dA * h + (dt_t * x_t)[:, :, None] * B_t[:, None, :]
                y = jnp.einsum('bdn,bn->bd', h, C_t) + D * x_t
                return (h, y)
            Bz, L, Di = x.shape
            h0 = jnp.zeros((Bz, Di, A.shape[1]), x.dtype)
            xs = (x.swapaxes(0, 1), dt.swapaxes(0, 1), Bm.swapaxes(0, 1), Cm.swapaxes(0, 1))
            _, ys = jax.lax.scan(step, h0, xs)
            return ys.swapaxes(0, 1) * jax.nn.silu(z)

        def _branch(x_in, z, conv_w, conv_b, xp_w, dt_w, dt_b, A_log, Dp):
            xc = _causal_conv_silu(x_in, conv_w, conv_b)
            proj = xc @ xp_w.T
            dt, Bm, Cm = jnp.split(proj, [DT_RANK, DT_RANK + D_STATE], axis=-1)
            dt = jax.nn.softplus(dt @ dt_w.T + dt_b)
            return _ssm_scan(xc, dt, -jnp.exp(A_log), Bm, Cm, Dp, z)
        xz = u @ in_proj_w.T
        x_in, z = jnp.split(xz, 2, axis=-1)
        y_fwd = _branch(x_in, z, fwd_conv_w, fwd_conv_b, fwd_x_proj_w, fwd_dt_w, fwd_dt_b, fwd_A_log, fwd_D)
        x_flip, z_flip = (x_in[:, ::-1, :], z[:, ::-1, :])
        y_bwd = _branch(x_flip, z_flip, bwd_conv_w, bwd_conv_b, bwd_x_proj_w, bwd_dt_w, bwd_dt_b, bwd_A_log, bwd_D)[:, ::-1, :]
        return (y_fwd + y_bwd) @ out_proj_w.T

    def _L0_ffn_ref(x, w_gate, w_up, w_down):
        import jax, jax.numpy as jnp
        import numpy as np
        DIM = 256
        HIDDEN = 768
        SCALE = 1.0 / 127.0

        def _dequant(w_int, dtype):
            return w_int.astype(dtype) * jnp.asarray(SCALE, dtype)
        wg = _dequant(w_gate, x.dtype)
        wu = _dequant(w_up, x.dtype)
        wd = _dequant(w_down, x.dtype)
        gate = jnp.einsum('bsd,hd->bsh', x, wg)
        up = jnp.einsum('bsd,hd->bsh', x, wu)
        h = jax.nn.silu(gate) * up
        return jnp.einsum('bsh,dh->bsd', h, wd)
    x = L0_attn_u
    x = x + _layernorm(_L0_attn_ref(_layernorm(x, axis=-1), L0_attn_in_proj_w, L0_attn_out_proj_w, L0_attn_fwd_conv_w, L0_attn_fwd_conv_b, L0_attn_fwd_x_proj_w, L0_attn_fwd_dt_w, L0_attn_fwd_dt_b, L0_attn_fwd_A_log, L0_attn_fwd_D, L0_attn_bwd_conv_w, L0_attn_bwd_conv_b, L0_attn_bwd_x_proj_w, L0_attn_bwd_dt_w, L0_attn_bwd_dt_b, L0_attn_bwd_A_log, L0_attn_bwd_D), axis=-1)
    x = x + _layernorm(_L0_ffn_ref(_layernorm(x, axis=-1), L0_ffn_w_gate, L0_ffn_w_up, L0_ffn_w_down), axis=-1)
    return x

_drawn_inputs = setup_inputs


def setup_inputs(seed=0):
    import zlib

    import numpy as np

    out = dict(_drawn_inputs(seed))
    spreads = {'L0_attn_fwd_D': (1.0, 0.2), 'L0_attn_bwd_D': (1.0, 0.2)}
    factors = {'L0_attn_fwd_x_proj_w': 27.996,
     'L0_attn_fwd_dt_w': 64.0,
     'L0_attn_fwd_dt_b': 64.0,
     'L0_attn_fwd_A_log': 64.0,
     'L0_attn_bwd_x_proj_w': 27.859,
     'L0_attn_bwd_dt_w': 64.0,
     'L0_attn_bwd_dt_b': 64.0,
     'L0_attn_bwd_A_log': 64.0}
    for name, (base, spread) in spreads.items():
        noise = np.random.default_rng([zlib.crc32(name.encode()), seed]).standard_normal(out[name].shape)
        drawn = base * np.exp(spread * noise) if base else spread * noise
        out[name] = jnp.asarray(drawn.astype(out[name].dtype))
    for name, factor in factors.items():
        out[name] = (out[name] * factor).astype(out[name].dtype)
    return out
```

```python
from contextlib import ExitStack

import concourse.bass as bass
from concourse import mybir

F32 = mybir.dt.float32
I32 = mybir.dt.int32
ALU = mybir.AluOpType
ACT = mybir.ActivationFunctionType

P = 128
BATCH, L, D_MODEL = 8, 512, 256
D_INNER, N_STATE, DT_RANK, D_CONV = 512, 16, 64, 4
HIDDEN = 768
J = D_INNER // P
K_MODEL = D_MODEL // P
T = L // P
H = HIDDEN // P
PROJ = DT_RANK + 2 * N_STATE
BIAS_ROW = PROJ
PAD = D_CONV - 1
STEPS = 2 * N_STATE
SLOTS = STEPS * J
RING = 4
LN_EPS = 1e-5
SCALE = 1.0 / 127.0
A_LOG_MAX = 84.0

TAIL, HERE, NEXT = -1, 0, 1


def pieces():
    out = [(0, "gate", 0, TAIL, 0)]
    out += [(1 + 1 * t, "z", t, HERE, 1) for t in range(T)]
    out += [(6 + 2 * k, "gated_t", k, TAIL, 1) for k in range(J)]
    out += [(14 + 3 * h, "out_proj", h, TAIL, 1) for h in range(2)]
    out += [(21, "norm_x1", 0, TAIL, 0)]
    out += [(24 + 1 * k, "x1_t", k, TAIL, 1) for k in range(K_MODEL)]
    for i in range(H):
        out += [(27 + 3 * i, "gate_proj", i, TAIL, 1), (28 + 3 * i, "up_proj", i, TAIL, 1)]
    out += [(46 + 3 * h, "down_proj", h, TAIL, 1) for h in range(2)]
    out += [(36 + 7 * j, "dt_bwd", j, HERE, 1) for j in range(J)]
    out += [(61, "norm_in", 0, NEXT, 0)]
    out += [(64 + k, "x_t", k, NEXT, 1) for k in range(K_MODEL)]
    for j in range(J):
        out += [(67 + 8 * j, "in_proj", j, NEXT, 1), (70 + 8 * j, "conv_fwd", j, NEXT, 1),
                (71 + 8 * j, "conv_bwd", j, NEXT, 1)]
    out += [(98 + 2 * r, "x_proj", r, NEXT, 1) for r in range(2)]
    out += [(102 + r, "c_t", r, NEXT, 1) for r in range(2)]
    out += [(105 + 6 * j, "dt_fwd", j, NEXT, 1) for j in range(J)]
    out += [(107 + 6 * t, "d_term", t, NEXT, 1) for t in range(T)]
    return sorted(out, key=lambda x: x[0])


PIECES = pieces()
BY_SLOT = {s: [x[1:] for x in PIECES if x[0] == s] for s in range(SLOTS)}
PER_ITERATION = sum(x[4] for x in PIECES)
FILLS = {row: [x for x in PIECES if x[3] == row] for row in (TAIL, HERE, NEXT)}
N_TAIL = sum(x[4] for x in FILLS[TAIL])
N_NEXT = sum(x[4] for x in FILLS[NEXT])
assert PER_ITERATION % 2 == 0


class Row:

    def __init__(self, number, i=None, step=0):
        self.number, self.i, self.step = number, i, step
        self.parity = number % 2

    def __add__(self, n):
        return Row(self.number + n, self.i, self.step)

    def count(self, per, more):
        fixed = per * self.number + more
        if self.i is None:
            return fixed if fixed > 0 else None
        return self.i * (per * self.step) + fixed

    def last(self):
        return self.i is None and self.number == BATCH - 1

    def index(self):
        return self.number if self.i is None else self.i * self.step + self.number


def fill_number(row, name, arg):
    for at, x in enumerate(PIECES):
        if x[1:3] == (name, arg):
            break
    whose = x[3]
    before = sum(y[4] for y in PIECES[:at])
    it = row + (-whose)
    if it.i is None and it.number == -1:
        before = sum(y[4] for y in PIECES[:at] if y[3] == NEXT)
        return 0, before
    if it.i is None and it.number == 0:
        return 0, N_NEXT + sum(y[4] for y in PIECES[:at] if y[3] != TAIL)
    if it.i is None and it.number == BATCH:
        before = sum(y[4] for y in PIECES[:at] if y[3] == TAIL)
        return 0, N_NEXT + PER_ITERATION * BATCH - N_TAIL - N_NEXT + before
    if it.i is None and it.number == BATCH - 1:
        before = sum(y[4] for y in PIECES[:at] if y[3] != NEXT)
        return 0, N_NEXT + PER_ITERATION * it.number - N_TAIL + before
    return PER_ITERATION, N_NEXT - N_TAIL + before, it


class Fill:

    def __init__(self, row, name, arg):
        got = fill_number(row, name, arg)
        self.it = got[2] if len(got) == 3 else Row(0)
        self.per, self.more = got[0], got[1]
        number = self.more + self.per * self.it.number
        self.bank = number % 2

    def order(self):
        return self.per * self.it.number + self.more

    def filled(self):
        return self.it.count(self.per, self.more + 1)

    def emptied(self, after=1):
        fixed = self.more + self.per * self.it.number
        half = (fixed - self.bank) // 2 + after
        if self.it.i is None or self.per == 0:
            return half if half > 0 else None
        return self.it.i * (self.per * self.it.step // 2) + half


def wait(eng, semaphore, value):
    if value is not None:
        eng.wait_ge(semaphore, value)


def walk(eng, unit, piece, drain):
    def iteration(row, tail, following):
        for slot in range(SLOTS):
            unit(row, slot)
            for name, arg, whose, _ in BY_SLOT[slot]:
                if (whose != TAIL or tail) and (whose != NEXT or following):
                    piece(row + whose, name, arg)
        drain(row)

    for _, name, arg, whose, _ in PIECES:
        if whose == NEXT:
            piece(Row(0), name, arg)
    iteration(Row(0), False, True)
    with eng.Fori(0, (BATCH - 2) // 2) as i:
        iteration(Row(1, i, 2), True, True)
        iteration(Row(2, i, 2), True, True)
    iteration(Row(BATCH - 1), True, False)
    for _, name, arg, whose, _ in PIECES:
        if whose == TAIL:
            piece(Row(BATCH - 1), name, arg)


def build(nc, a, out):
    ctx = ExitStack()
    with ctx:
        def sb(name, shape, dt=F32):
            return ctx.enter_context(nc.sbuf_tensor(name, shape, dt))

        def sem(name):
            return ctx.enter_context(nc.semaphore(name))

        decay = ctx.enter_context(nc.psum_tensor("decay", [P, RING, L], F32))
        h_t = ctx.enter_context(nc.psum_tensor("h_t", [P, 2, D_INNER], F32))
        banks = ctx.enter_context(nc.psum_tensor("banks", [P, 2, 512], F32))

        w_in = sb("w_in", [P, K_MODEL, 2 * D_INNER])
        w_conv = sb("w_conv", [P, 2, J, D_CONV])
        b_conv = sb("b_conv", [P, 2, J])
        conv_diag = sb("conv_diag", [P, 2, J, D_CONV, P])
        w_skip = sb("w_skip", [P, 2, J])
        skip_diag = sb("skip_diag", [P, 2, J, P])
        w_xproj = sb("w_xproj", [P, 2, J, PROJ])
        w_dt = sb("w_dt", [PROJ + 1, 2, D_INNER])
        a_neg = sb("a_neg", [P, 2, J, N_STATE])
        w_out = sb("w_out", [P, J, D_MODEL])
        w_gate = sb("w_gate", [P, K_MODEL, HIDDEN])
        w_up = sb("w_up", [P, K_MODEL, HIDDEN])
        w_down = sb("w_down", [P, H, D_MODEL])
        ident = sb("ident", [P, P])
        eps = sb("eps", [P, 1])
        marker = sb("marker", [P, 1])

        x = sb("x", [P, T, D_MODEL])
        x1 = sb("x1", [P, T, D_MODEL])
        normed = sb("normed", [P, T, D_MODEL])
        normed_t = sb("normed_t", [P, K_MODEL, L])
        stats = sb("stats", [P, T, 6])
        mean_var = sb("mean_var", [P, T, 2])
        log_var = sb("log_var", [P, T])
        rstd = sb("rstd", [P, T])
        x_in = sb("x_in", [P, 2, L + 2 * PAD])
        xc = sb("xc", [P, 2, J, L])
        proj = sb("proj", [PROJ + 1, 2, L])
        c_nat = sb("c_nat", [P, 2, 2, T, N_STATE])
        sp_e = sb("sp_e", [P, L])
        sp_log = sb("sp_log", [P, L])
        sp_w = sb("sp_w", [P, L])
        dt = sb("dt", [P, 2, J, L])
        dtx = sb("dtx", [P, 2, J, L])
        b_wide = sb("b_wide", [P, RING, L])
        drive = sb("drive", [P, RING, L])
        h = sb("h", [P, 2, J, L])
        acc = sb("acc", [P, 2, T, D_INNER])
        z = sb("z", [P, T, D_INNER])
        hidden = sb("hidden", [P, H, L])
        gated_t = hidden[:, 0:J, :]
        gate_i32 = acc[:, :, :, :].rearrange("p a t d -> p (a t d)")[:, 0:K_MODEL * HIDDEN].bitcast(I32)
        up_i32 = acc[:, :, :, :].rearrange("p a t d -> p (a t d)")[:, K_MODEL * HIDDEN:2 * K_MODEL * HIDDEN].bitcast(I32)
        down_i32 = hidden[:, :, :].rearrange("p a b -> p (a b)")[:, 0:H * D_MODEL].bitcast(I32)
        b_rows = nc.dram_tensor("b_rows", (2, 2, N_STATE, L), F32, kind="Internal").ap()

        w_in_loaded, w_conv_loaded, w_rest_loaded, w_int_loaded = map(sem, ("w_in_loaded", "w_conv_loaded", "w_rest_loaded", "w_int_loaded"))
        ident_zeroed, ident_made, consts_made = map(sem, ("ident_zeroed", "ident_made", "consts_made"))
        rows_made, diag_made = map(sem, ("rows_made", "diag_made"))
        a_min, a_exp, a_made, int_cast = map(sem, ("a_min", "a_exp", "a_made", "int_cast"))
        x_loaded, x1_loaded, out_stored = map(sem, ("x_loaded", "x1_loaded", "out_stored"))
        decay_made, drive_made, scan_made = map(sem, ("decay_made", "drive_made", "scan_made"))
        reset_made = sem("reset_made")
        h_t_made, acc_made = map(sem, ("h_t_made", "acc_made"))
        b_wide_loaded = [sem(f"b_wide_loaded{k}") for k in range(RING)]
        b_stored = [sem(f"b_stored{r}") for r in range(2)]
        bank_filled = sem("bank_filled")
        bank_emptied = [sem(f"bank_emptied{k}") for k in range(2)]
        abs_made, exp_made, log_made, one_plus_made = map(sem, ("abs_made", "exp_made", "log_made", "one_plus_made"))
        dt_made, dtx_made = map(sem, ("dt_made", "dtx_made"))
        gated = sem("gated")
        sig_made = sem("sig_made")
        ln = {k: {e: sem(f"ln_{k}_{e}") for e in ("stats", "mean", "log", "rstd", "normed", "added")} for k in ("in", "attn", "x1", "ffn")}

        BANK = lambda f: banks[:, f.bank, :]

        def emptied(eng, row, *needs, free=None):
            for k in range(2):
                uses = [f for f in (Fill(row, name, arg) for name, arg in needs) if f.bank == k]
                if free is not None and free.bank == k:
                    wait(eng, bank_emptied[k], free.emptied(after=0))
                elif uses:
                    eng.wait_ge(bank_emptied[k], max(uses, key=Fill.order).emptied())

        block = ctx.enter_context(nc.Block())

        @block.sync
        def _(sp):
            def load_x(row):
                number = row.index()
                wait(sp, ln["in"]["normed"], row.count(1, 0))
                sp.dma_start(x[:, :, :], a["u"][bass.ds(number, 1)].rearrange("b (t p) d -> p (b t) d", p=P)).then_inc(x_loaded, 16)

            def load_x1(row):
                number = row.index()
                wait(sp, out_stored, row.count(32, 0))
                sp.dma_start(x1[:, :, :], a["u"][bass.ds(number, 1)].rearrange("b (t p) d -> p (b t) d", p=P)).then_inc(x1_loaded, 16)

            def load_b(row, step):
                r, n = divmod(step, N_STATE)
                if n == 0 and row.i is None:
                    sp.wait_ge(b_stored[r], row.count(16, 16))
                wait(sp, drive_made, row.count(SLOTS, J * (step - RING + 1)))
                sp.dma_start(b_wide[:, step % RING, :], b_rows[row.parity, r, n:n + 1, :].partition_broadcast(P)
                             ).then_inc(b_wide_loaded[step % RING], 16)

            sp.dma_start(x[:, :, :], a["u"][0:1].rearrange("b (t p) d -> p (b t) d", p=P)).then_inc(x_loaded, 16)
            sp.dma_start(w_in[:, :, :], a["in_proj_w"].rearrange("(k p) n -> p k n", p=P)).then_inc(w_in_loaded, 16)
            for r, d in enumerate(("fwd", "bwd")):
                sp.dma_start(w_xproj[:, r, :, :], a[f"{d}_x_proj_w"].rearrange("(j p) n -> p j n", p=P)).then_inc(w_rest_loaded, 16)
                sp.dma_start(w_dt[0:DT_RANK, r, :], a[f"{d}_dt_w"]).then_inc(w_rest_loaded, 16)
                sp.dma_start(w_dt[BIAS_ROW:BIAS_ROW + 1, r, :], a[f"{d}_dt_b"].rearrange("(o n) -> o n", o=1)).then_inc(w_rest_loaded, 16)
            sp.dma_start(w_out[:, :, :], a["out_proj_w"].rearrange("(j p) n -> p j n", p=P)).then_inc(w_rest_loaded, 16)

            def unit(row, slot):
                step, j = divmod(slot, J)
                if j == 0 and step == 0:
                    load_b(row, 0)
                    load_b(row, 1)
                    load_b(row, 2)
                if j == 0 and step + 3 < STEPS:
                    load_b(row, step + 3)

            def piece(row, name, arg):
                if name == "x_proj":
                    emptied(sp, row, ("x_proj", arg))
                    for k in range(RING):
                        wait(sp, b_wide_loaded[k], row.count(16 * STEPS // RING, -16 * STEPS // RING))
                    sp.dma_start(b_rows[row.parity, arg], proj[DT_RANK:DT_RANK + N_STATE, arg, :]).then_inc(b_stored[arg], 16)
                if name == "gate":
                    load_x1(row)
                if name == "z" and arg == 0 and not row.last():
                    load_x(row + 1)
                if name == "down_proj":
                    number = row.index()
                    sp.wait_ge(ln["ffn"]["added"], row.count(2, arg + 1))
                    sp.dma_start(out[bass.ds(number, 1), arg * 2 * P:(arg + 1) * 2 * P, :].rearrange("b (t p) d -> p (b t) d", p=P),
                                 x1[:, 2 * arg:2 * arg + 2, :]).then_inc(out_stored, 16)

            walk(sp, unit, piece, lambda row: None)
            sp.wait_ge(out_stored, 32 * BATCH)

        @block.gpsimd
        def _(pool):
            pool.memset(ident[:, :], 0.0).then_inc(ident_zeroed, 1)
            pool.wait_ge(ident_zeroed, 1)
            pool.affine_select(out=ident[:, :], in_=ident[:, :], compare_op=ALU.not_equal, fill=1.0, base=0,
                               pattern=[[-1, P]], channel_multiplier=1).then_inc(ident_made, 1)
            pool.memset(eps[:, :], LN_EPS)
            pool.memset(x_in[:, :, 0:PAD], 0.0)
            pool.memset(x_in[:, :, L + PAD:L + 2 * PAD], 0.0).then_inc(consts_made, 1)

            def unit(row, slot):
                step, j = divmod(slot, J)
                r = step // N_STATE
                if slot == SLOTS - RING * J and not row.last():
                    for k in range(2):
                        pool.wait_ge(b_stored[k], (row + 1).count(16, 16))
                if j == 0:
                    pool.wait_ge(b_wide_loaded[step % RING], row.count(16 * STEPS // RING, 16 * (step // RING + 1)))
                if step % N_STATE == 0:
                    pool.wait_ge(dtx_made, row.count(2 * J, J * r + j + 1))
                wait(pool, scan_made, row.count(SLOTS, slot + 1 - RING))
                pool.tensor_tensor(drive[:, slot % RING, :], dtx[:, r, j, :], b_wide[:, step % RING, :], ALU.mult).then_inc(drive_made, 1)

            def piece(row, name, arg):
                if name not in ("dt_fwd", "dt_bwd"):
                    return
                r = int(name == "dt_bwd")
                made = row.count(2 * J, J * r + arg + 1)
                emptied(pool, row, (name, arg))
                wait(pool, decay_made, row.count(SLOTS, -SLOTS + SLOTS // 2 * (r + 1) - J + arg + 1))
                pool.tensor_tensor(dt[:, r, arg, :], sp_log[:, :], sp_w[:, :], ALU.subtract).then_inc(dt_made, 1)
                wait(pool, drive_made, row.count(SLOTS, -SLOTS + SLOTS // 2 * (r + 1) - J + arg + 1))
                pool.wait_ge(dt_made, made)
                pool.tensor_tensor(dtx[:, r, arg, :], dt[:, r, arg, :], xc[:, r, arg, :], ALU.mult).then_inc(dtx_made, 1)

            walk(pool, unit, piece, lambda row: None)

        @block.scalar
        def _(act):
            for r, d in enumerate(("fwd", "bwd")):
                act.dma_start(w_conv[:, r, :, :], a[f"{d}_conv_w"]).then_inc(w_conv_loaded, 16)
                act.dma_start(b_conv[:, r, :], a[f"{d}_conv_b"]).then_inc(w_conv_loaded, 16)
                act.dma_start(w_skip[:, r, :], a[f"{d}_D"]).then_inc(w_conv_loaded, 16)
                act.dma_start(a_neg[:, r, :, :], a[f"{d}_A_log"].rearrange("(j p) n -> p j n", p=P)).then_inc(w_conv_loaded, 16)
            act.dma_start(gate_i32.rearrange("p (k n) -> p k n", k=K_MODEL), a["w_gate"].rearrange("(k p) n -> p k n", p=P)).then_inc(w_int_loaded, 16)
            act.dma_start(up_i32.rearrange("p (k n) -> p k n", k=K_MODEL), a["w_up"].rearrange("(k p) n -> p k n", p=P)).then_inc(w_int_loaded, 16)
            act.dma_start(down_i32.rearrange("p (i n) -> p i n", i=H), a["w_down"].rearrange("(i p) n -> p i n", p=P)).then_inc(w_int_loaded, 16)
            act.wait_ge(consts_made, 1)
            act.wait_ge(a_min, 1)
            act.activation(a_neg[:, :, :, :], a_neg[:, :, :, :], ACT.Exp).then_inc(a_exp, 1)

            def unit(row, slot):
                step, j = divmod(slot, J)
                r, n = divmod(step, N_STATE)
                if n == 0:
                    act.wait_ge(dt_made, row.count(2 * J, J * r + j + 1))
                if slot == 0 and row.i is None and row.number == 0:
                    act.wait_ge(a_made, 1)
                wait(act, scan_made, row.count(SLOTS, slot + 1 - RING))
                lo = 1 - r
                act.activation(decay[:, slot % RING, lo:lo + L - 1], dt[:, r, j, lo:lo + L - 1], ACT.Exp,
                               scale=a_neg[:, r, j, n:n + 1]).then_inc(decay_made, 1)

            def read_bank(row, name, arg):
                f = Fill(row, name, arg)
                act.wait_ge(bank_filled, f.filled())
                return f, bank_emptied[f.bank]

            def rstd_of(kind, count, tiles):
                act.wait_ge(ln[kind]["mean"], count)
                act.activation(log_var[:, tiles], mean_var[:, tiles, 1], ACT.Ln, bias=eps[:, 0:1]).then_inc(ln[kind]["log"], 1)
                act.wait_ge(ln[kind]["log"], count)
                act.activation(rstd[:, tiles], log_var[:, tiles], ACT.Exp, scale=-0.5).then_inc(ln[kind]["rstd"], 1)

            def piece(row, name, arg):
                if name in ("norm_in", "norm_x1"):
                    rstd_of(name[5:], row.count(1, 1), slice(0, T))
                elif name in ("out_proj", "down_proj"):
                    rstd_of("attn" if name == "out_proj" else "ffn", row.count(2, arg + 1), slice(2 * arg, 2 * arg + 2))
                elif name in ("x_t", "x1_t"):
                    f, done = read_bank(row, name, arg)
                    act.activation(normed_t[:, arg, :], BANK(f), ACT.Copy).then_inc(done, 1)
                elif name == "in_proj":
                    f, done = read_bank(row, name, arg)
                    act.activation(x_in[:, arg % 2, PAD:PAD + L], BANK(f), ACT.Copy).then_inc(done, 1)
                elif name in ("conv_fwd", "conv_bwd"):
                    r = int(name == "conv_bwd")
                    wait(act, dtx_made, row.count(2 * J, -J + J * r))
                    f, done = read_bank(row, name, arg)
                    act.activation(xc[:, r, arg, :], BANK(f), ACT.Silu, bias=b_conv[:, r, arg:arg + 1]).then_inc(done, 1)
                elif name == "x_proj":
                    wait(act, b_stored[arg], row.count(16, 0))
                    f, done = read_bank(row, name, arg)
                    act.activation(proj[0:PROJ, arg, :], banks[0:PROJ, f.bank, :], ACT.Copy).then_inc(done, 1)
                elif name == "c_t":
                    wait(act, acc_made, row.count(SLOTS, -SLOTS))
                    f, done = read_bank(row, name, arg)
                    act.activation(c_nat[:, row.parity, arg, :, :],
                                   banks[:, f.bank, 0:T * PROJ].rearrange("p (t c) -> p t c", t=T)[:, :, DT_RANK + N_STATE:PROJ],
                                   ACT.Copy).then_inc(done, 1)
                elif name == "d_term":
                    if row.i is None and row.number == 0:
                        act.wait_ge(int_cast, 1)
                    f, done = read_bank(row, name, arg)
                    act.activation(acc[:, row.parity, arg, :], BANK(f), ACT.Copy).then_inc(done, 1)
                elif name in ("dt_fwd", "dt_bwd"):
                    r = int(name == "dt_bwd")
                    made = row.count(2 * J, J * r + arg + 1)
                    wait(act, dt_made, row.count(2 * J, J * r + arg))
                    f, _ = read_bank(row, name, arg)
                    act.activation(sp_e[:, :], BANK(f), ACT.Abs).then_inc(abs_made, 1)
                    act.wait_ge(abs_made, made)
                    act.activation(sp_e[:, :], sp_e[:, :], ACT.Exp, scale=-1.0).then_inc(exp_made, 1)
                    act.wait_ge(exp_made, made)
                    act.activation(sp_w[:, :], sp_e[:, :], ACT.Copy, bias=1.0).then_inc(one_plus_made, 1)
                    act.activation(sp_log[:, :], sp_e[:, :], ACT.Ln, bias=1.0).then_inc(log_made, 1)
                elif name == "z":
                    wait(act, gated, row.count(T, 0))
                    f, done = read_bank(row, name, arg)
                    act.activation(z[:, arg, :], BANK(f), ACT.Silu).then_inc(done, 1)
                elif name == "gated_t":
                    f, done = read_bank(row, name, arg)
                    act.activation(gated_t[:, arg, :], BANK(f), ACT.Copy).then_inc(done, 1)
                elif name == "gate_proj":
                    f, done = read_bank(row, name, arg)
                    act.activation(hidden[:, arg, :], BANK(f), ACT.Silu, scale=SCALE).then_inc(done, 1)

            walk(act, unit, piece, lambda row: None)

        @block.tensor
        def _(pe):
            def fill_bank(row, name, arg, *needs):
                f = Fill(row, name, arg)
                emptied(pe, row, *needs, free=f)
                return f

            def transpose_step(row, step, t):
                number = J * step + t
                pe.wait_ge(scan_made, row.count(SLOTS, J * step + J))
                wait(pe, acc_made, row.count(SLOTS, number + 1 - 2))
                for j in range(J):
                    last = pe.transpose(h_t[:, number % 2, j * P:(j + 1) * P], h[:, step % 2, j, t * P:(t + 1) * P], ident[:, :])
                last.then_inc(h_t_made, 1)

            def unit(row, slot):
                step, j = divmod(slot, J)
                if step:
                    transpose_step(row, step - 1, j)

            def drain(row):
                for t in range(T):
                    transpose_step(row, STEPS - 1, t)

            pe.wait_ge(ident_made, 1)
            pe.wait_ge(consts_made, 1)
            pe.wait_ge(rows_made, 1)
            pe.wait_ge(w_in_loaded, 16)

            def piece(row, name, arg):
                if name in ("x_t", "x1_t"):
                    pe.wait_ge(ln["in" if name == "x_t" else "x1"]["normed"], row.count(1, 1))
                    f = fill_bank(row, name, arg)
                    for t in range(T):
                        last = pe.transpose(banks[:, f.bank, t * P:(t + 1) * P], normed[:, t, arg * P:(arg + 1) * P], ident[:, :])
                elif name == "in_proj":
                    f = fill_bank(row, name, arg, *[("x_t", k) for k in range(K_MODEL)])
                    for k in range(K_MODEL):
                        last = pe.matmul(BANK(f), w_in[:, k, arg * P:(arg + 1) * P], normed_t[:, k, :], start=(k == 0), stop=(k == K_MODEL - 1))
                elif name in ("conv_fwd", "conv_bwd"):
                    r = int(name == "conv_bwd")
                    if row.i is None and row.number == 0 and arg == 0:
                        pe.wait_ge(diag_made, 1)
                    f = fill_bank(row, name, arg, ("in_proj", arg))
                    for tap in range(D_CONV):
                        at = tap if r == 0 else 2 * PAD - tap
                        last = pe.matmul(BANK(f), conv_diag[:, r, arg, tap, :], x_in[:, arg % 2, at:at + L],
                                         start=(tap == 0), stop=(tap == D_CONV - 1))
                elif name == "x_proj":
                    if row.i is None and row.number == 0:
                        pe.wait_ge(w_rest_loaded, 16 * 7)
                    f = fill_bank(row, name, arg, *[("conv_bwd" if arg else "conv_fwd", j) for j in range(J)])
                    for j in range(J):
                        last = pe.matmul(banks[0:PROJ, f.bank, :], w_xproj[:, arg, j, :], xc[:, arg, j, :], start=(j == 0), stop=(j == J - 1))
                elif name == "c_t":
                    f = fill_bank(row, name, arg, ("x_proj", arg))
                    for t in range(T):
                        last = pe.transpose(banks[:, f.bank, t * PROJ:(t + 1) * PROJ], proj[0:PROJ, arg, t * P:(t + 1) * P], ident[0:PROJ, 0:PROJ])
                elif name in ("dt_fwd", "dt_bwd"):
                    r = int(name == "dt_bwd")
                    f = fill_bank(row, name, arg, ("x_proj", r))
                    last = pe.matmul(BANK(f), w_dt[:, r, arg * P:(arg + 1) * P], proj[:, r, :], start=True, stop=True)
                elif name == "d_term":
                    f = fill_bank(row, name, arg, *[("conv_bwd", j) for j in range(J)])
                    for j in range(J):
                        for r in range(2):
                            last = pe.matmul(banks[:, f.bank, j * P:(j + 1) * P], xc[:, r, j, arg * P:(arg + 1) * P], skip_diag[:, r, j, :],
                                             start=(r == 0), stop=(r == 1))
                elif name == "z":
                    f = fill_bank(row, name, arg)
                    for k in range(K_MODEL):
                        last = pe.matmul(BANK(f), normed_t[:, k, arg * P:(arg + 1) * P], w_in[:, k, D_INNER:2 * D_INNER],
                                         start=(k == 0), stop=(k == K_MODEL - 1))
                elif name == "gated_t":
                    pe.wait_ge(gated, row.count(T, T))
                    f = fill_bank(row, name, arg)
                    for t in range(T):
                        last = pe.transpose(banks[:, f.bank, t * P:(t + 1) * P], acc[:, row.parity, t, arg * P:(arg + 1) * P], ident[:, :])
                elif name == "out_proj":
                    f = fill_bank(row, name, arg, *[("gated_t", k) for k in range(J)])
                    for t in (2 * arg, 2 * arg + 1):
                        for k in range(J):
                            last = pe.matmul(banks[:, f.bank, (t % 2) * D_MODEL:(t % 2 + 1) * D_MODEL], gated_t[:, k, t * P:(t + 1) * P],
                                             w_out[:, k, :], start=(k == 0), stop=(k == J - 1))
                elif name in ("gate_proj", "up_proj"):
                    f = fill_bank(row, name, arg, *[("x1_t", k) for k in range(K_MODEL)])
                    w = w_gate if name == "gate_proj" else w_up
                    for k in range(K_MODEL):
                        last = pe.matmul(BANK(f), w[:, k, arg * P:(arg + 1) * P], normed_t[:, k, :], start=(k == 0), stop=(k == K_MODEL - 1))
                elif name == "down_proj":
                    f = fill_bank(row, name, arg, *[("up_proj", i) for i in range(H)])
                    for t in (2 * arg, 2 * arg + 1):
                        for i in range(H):
                            last = pe.matmul(banks[:, f.bank, (t % 2) * D_MODEL:(t % 2 + 1) * D_MODEL], hidden[:, i, t * P:(t + 1) * P],
                                             w_down[:, i, :], start=(i == 0), stop=(i == H - 1))
                else:
                    return
                last.then_inc(bank_filled, 1)

            walk(pe, unit, piece, drain)

        @block.vector
        def _(dve):
            dve.memset(proj[BIAS_ROW:BIAS_ROW + 1, :, :], 1.0)
            dve.memset(w_dt[DT_RANK:PROJ, :, :], 0.0).then_inc(rows_made, 1)
            dve.wait_ge(w_conv_loaded, 16 * 8)
            dve.tensor_scalar(a_neg[:, :, :, :], a_neg[:, :, :, :], A_LOG_MAX, None, ALU.min).then_inc(a_min, 1)

            def weights():
                dve.wait_ge(ident_made, 1)
                for j in range(J):
                    for r in range(2):
                        for tap in range(D_CONV):
                            dve.tensor_scalar(conv_diag[:, r, j, tap, :], ident[:, :], w_conv[:, r, j, tap:tap + 1], None, ALU.mult)
                        last = dve.tensor_scalar(skip_diag[:, r, j, :], ident[:, :], w_skip[:, r, j:j + 1], None, ALU.mult)
                last.then_inc(diag_made, 1)
                dve.wait_ge(a_exp, 1)
                dve.tensor_scalar(a_neg[:, :, :, :], a_neg[:, :, :, :], -1.0, None, ALU.mult).then_inc(a_made, 1)
                dve.wait_ge(w_int_loaded, 16 * 3)
                flat = lambda w: w[:, :, :].rearrange("p a b -> p (a b)")
                dve.tensor_copy(flat(w_gate), gate_i32)
                dve.tensor_copy(flat(w_up), up_i32)
                dve.tensor_copy(flat(w_down), down_i32).then_inc(int_cast, 1)

            def scan(row, slot):
                step, j = divmod(slot, J)
                r, n = divmod(step, N_STATE)
                bank = slot % RING
                dve.wait_ge(decay_made, row.count(SLOTS, slot + 1))
                if n == 0:
                    first = 0 if r == 0 else L - 1
                    dve.memset(decay[:, bank, first:first + 1], 0.0).then_inc(reset_made, 1)
                    dve.wait_ge(reset_made, row.count(2 * J, J * r + j + 1))
                dve.wait_ge(drive_made, row.count(SLOTS, slot + 1))
                wait(dve, h_t_made, row.count(SLOTS, J * (step - 1)))
                order = slice(0, L) if r == 0 else slice(L - 1, None, -1)
                dve.tensor_tensor_scan(h[:, step % 2, j, order], decay[:, bank, order], drive[:, bank, order], 0.0,
                                       ALU.mult, ALU.add).then_inc(scan_made, 1)

            def accumulate(row, step, t):
                r, n = divmod(step, N_STATE)
                number = J * step + t
                if n == 0:
                    emptied(dve, row, ("c_t", r), *([("d_term", t)] if step == 0 else []))
                dve.wait_ge(h_t_made, row.count(SLOTS, number + 1))
                if step:
                    dve.wait_ge(acc_made, row.count(SLOTS, number + 1 - T))
                dve.scalar_tensor_tensor(out=acc[:, row.parity, t, :], in0=h_t[:, number % 2, :], scalar=c_nat[:, row.parity, r, t, n:n + 1],
                                         in1=acc[:, row.parity, t, :], op0=ALU.mult, op1=ALU.add).then_inc(acc_made, 1)

            def unit(row, slot):
                step, j = divmod(slot, J)
                scan(row, slot)
                if step:
                    accumulate(row, step - 1, j)

            def drain(row):
                for t in range(T):
                    accumulate(row, STEPS - 1, t)

            def layernorm(kind, count, src, tiles):
                for k, t in enumerate(tiles):
                    last = dve.bn_stats(stats[:, t, :], src(k))
                last.then_inc(ln[kind]["stats"], 1)
                dve.wait_ge(ln[kind]["stats"], count)
                dve.memset(marker[:, :], 0.0)
                for t in tiles:
                    last = dve.bn_aggr(mean_var[:, t, :], stats[:, t, :])
                last.then_inc(ln[kind]["mean"], 1)
                dve.wait_ge(ln[kind]["rstd"], count)
                for k, t in enumerate(tiles):
                    last = dve.tensor_scalar(normed[:, t, :], src(k), mean_var[:, t, 0:1], rstd[:, t:t + 1], ALU.subtract, ALU.mult)
                return last

            def piece(row, name, arg):
                if name == "norm_in":
                    dve.wait_ge(x_loaded, row.count(16, 16))
                    if not (row.i is None and row.number == 0):
                        wait(dve, ln["ffn"]["added"], row.count(2, -2))
                    layernorm("in", row.count(1, 1), lambda t: x[:, t, :], range(T)).then_inc(ln["in"]["normed"], 1)
                    if row.i is None and row.number == 0:
                        weights()
                elif name == "d_term":
                    pass
                elif name in ("dt_fwd", "dt_bwd"):
                    r = int(name == "dt_bwd")
                    made = row.count(2 * J, J * r + arg + 1)
                    f = Fill(row, name, arg)
                    dve.wait_ge(one_plus_made, made)
                    dve.wait_ge(log_made, made)
                    dve.scalar_tensor_tensor(out=sp_w[:, :], in0=sp_w[:, :], scalar=1.0, in1=sp_e[:, :], op0=ALU.subtract, op1=ALU.subtract)
                    dve.scalar_tensor_tensor(out=sp_log[:, :], in0=BANK(f), scalar=0.0, in1=sp_log[:, :], op0=ALU.max, op1=ALU.add
                                             ).then_inc(bank_emptied[f.bank], 1)
                elif name == "gate":
                    emptied(dve, row, *[("z", t) for t in range(T)])
                    dve.wait_ge(acc_made, row.count(SLOTS, SLOTS))
                    for t in range(T):
                        dve.tensor_tensor(acc[:, row.parity, t, :], acc[:, row.parity, t, :], z[:, t, :], ALU.mult).then_inc(gated, 1)
                elif name in ("out_proj", "down_proj"):
                    kind = "attn" if name == "out_proj" else "ffn"
                    count = row.count(2, arg + 1)
                    tiles = range(2 * arg, 2 * arg + 2)
                    f = Fill(row, name, arg)
                    dve.wait_ge(bank_filled, f.filled())
                    layernorm(kind, count, lambda k: banks[:, f.bank, k * D_MODEL:(k + 1) * D_MODEL], tiles).then_inc(bank_emptied[f.bank], 1)
                    dve.wait_ge(bank_emptied[f.bank], f.emptied())
                    if name == "out_proj":
                        dve.wait_ge(x1_loaded, row.count(16, 16))
                    dve.tensor_tensor(x1[:, 2 * arg:2 * arg + 2, :], x1[:, 2 * arg:2 * arg + 2, :], normed[:, 2 * arg:2 * arg + 2, :], ALU.add
                                      ).then_inc(ln[kind]["added"], 1)
                elif name == "norm_x1":
                    dve.wait_ge(ln["attn"]["added"], row.count(2, 2))
                    layernorm("x1", row.count(1, 1), lambda t: x1[:, t, :], range(T)).then_inc(ln["x1"]["normed"], 1)
                elif name == "up_proj":
                    f = Fill(row, name, arg)
                    dve.wait_ge(bank_filled, f.filled())
                    emptied(dve, row, ("gate_proj", arg))
                    dve.scalar_tensor_tensor(out=hidden[:, arg, :], in0=BANK(f), scalar=SCALE * SCALE, in1=hidden[:, arg, :],
                                             op0=ALU.mult, op1=ALU.mult).then_inc(bank_emptied[f.bank], 1)

            walk(dve, unit, piece, drain)


_NAMES = {
    "u": "L0_attn_u", "in_proj_w": "L0_attn_in_proj_w", "out_proj_w": "L0_attn_out_proj_w",
    "fwd_conv_w": "L0_attn_fwd_conv_w", "fwd_conv_b": "L0_attn_fwd_conv_b", "fwd_x_proj_w": "L0_attn_fwd_x_proj_w",
    "fwd_dt_w": "L0_attn_fwd_dt_w", "fwd_dt_b": "L0_attn_fwd_dt_b", "fwd_A_log": "L0_attn_fwd_A_log", "fwd_D": "L0_attn_fwd_D",
    "bwd_conv_w": "L0_attn_bwd_conv_w", "bwd_conv_b": "L0_attn_bwd_conv_b", "bwd_x_proj_w": "L0_attn_bwd_x_proj_w",
    "bwd_dt_w": "L0_attn_bwd_dt_w", "bwd_dt_b": "L0_attn_bwd_dt_b", "bwd_A_log": "L0_attn_bwd_A_log", "bwd_D": "L0_attn_bwd_D",
    "w_gate": "L0_ffn_w_gate", "w_up": "L0_ffn_w_up", "w_down": "L0_ffn_w_down",
}
_TRANSPOSED = ("in_proj_w", "out_proj_w", "fwd_x_proj_w", "bwd_x_proj_w", "fwd_dt_w", "bwd_dt_w", "w_gate", "w_up", "w_down")
_CHANNELS = ("fwd_conv_w", "fwd_conv_b", "fwd_D", "bwd_conv_w", "bwd_conv_b", "bwd_D")


def kernel(**inputs):
    import numpy as _np
    import concourse.bacc as _bacc
    from concourse import mybir as _mybir
    from concourse.bass_utils import run_bass_kernel_spmd as _run

    nc = _bacc.Bacc("TRN2", target_bir_lowering=False, num_devices=1)
    arrays, args = {}, {}
    for name, given in _NAMES.items():
        v = _np.asarray(inputs[given])
        if name in _TRANSPOSED:
            v = v.T
        elif name in _CHANNELS:
            v = _np.moveaxis(v.reshape(J, P, *[n for n in v.shape[1:] if n > 1]), 0, 1)
        v = _np.ascontiguousarray(v)
        arrays[f"in_{name}"] = v
        args[name] = nc.dram_tensor(f"in_{name}", v.shape, _mybir.dt.from_np(v.dtype), kind="ExternalInput").ap()
    out = nc.dram_tensor("out", (BATCH, L, D_MODEL), _mybir.dt.float32, kind="ExternalOutput").ap()
    build(nc, args, out)
    r = _run(nc, [arrays], core_ids=[0])
    return r.results[0]["out"]
```

```python
from contextlib import ExitStack

import concourse.bass as bass
from concourse import mybir

F32 = mybir.dt.float32
I32 = mybir.dt.int32
ALU = mybir.AluOpType
ACT = mybir.ActivationFunctionType

P = 128
BATCH, L, D_MODEL = 8, 512, 256
D_INNER, N_STATE, DT_RANK, D_CONV = 512, 16, 64, 4
HIDDEN = 768
J = D_INNER // P
K_MODEL = D_MODEL // P
T = L // P
H = HIDDEN // P
PROJ = DT_RANK + 2 * N_STATE
BIAS_ROW = PROJ
PAD = D_CONV - 1
STEPS = 2 * N_STATE
SLOTS = STEPS * J
RING = 4
LN_EPS = 1e-5
SCALE = 1.0 / 127.0
A_LOG_MAX = 84.0

TAIL, HERE, NEXT = -1, 0, 1


def pieces():
    def at(name, whose, slots, fills=1):
        return [(slot, name, arg, whose, fills) for arg, slot in enumerate(slots)]

    out = at("gate", TAIL, [0], 0)
    out += at("dt_bwd", HERE, [1, 3, 30, 56])
    out += at("gated_t", TAIL, [5, 7, 9, 11])
    out += at("out_proj", TAIL, [14, 16])
    out += at("z", HERE, [18, 20, 22, 24])
    out += at("norm_x1", TAIL, [21], 0)
    out += at("x1_t", TAIL, [26, 28])
    out += at("gate_proj", TAIL, [32, 34, 40, 42, 48, 50])
    out += at("up_proj", TAIL, [36, 38, 44, 46, 52, 54])
    out += at("down_proj", TAIL, [58, 60])
    out += at("norm_in", NEXT, [62], 0)
    out += at("x_t", NEXT, [67, 69])
    out += at("in_proj", NEXT, [72, 74, 80, 86])
    out += at("conv_fwd", NEXT, [76, 82, 88, 92])
    out += at("conv_bwd", NEXT, [78, 84, 90, 94])
    out += at("x_proj", NEXT, [97, 99])
    out += at("c_t", NEXT, [101, 103])
    out += at("dt_fwd", NEXT, [105, 109, 113, 117])
    out += at("d_term", NEXT, [107, 111, 115, 119])
    return sorted(out, key=lambda x: x[0])


LAGS = {
    "pe": {"": (0, {})},
    "sp": {"": (3, {"gate": 0, "z": 0, "down_proj": 5})},
    "act": {"": (3, {"z0": 5, "z2": 5, "conv_fwd": 5, "gate_proj0": 5, "gate_proj2": 5, "gate_proj4": 5,
                     "norm_in": 4, "norm_x1": 4, "out_proj": 5, "down_proj": 5})},
    "dve": {"stats": (1, {"norm_x1": 0, "norm_in": 0}),
            "": (2, {"gate": 0, "norm_in": 3, "norm_x1": 2, "dt_fwd": 3, "dt_bwd": 3, "out_proj": 3, "down_proj": 3})},
    "pool": {"": (7, {})},
}
LAYERNORMS = ("in", "attn", "x1", "ffn")
STATS = ("norm_in", "norm_x1", "out_proj", "down_proj")


def parts(engine):
    out = []
    for part, (lag, by_name) in LAGS[engine].items():
        for slot, name, arg, whose, _ in PIECES:
            if part and name not in STATS:
                continue
            lag_here = by_name.get(f"{name}{arg}", by_name.get(name, lag))
            out.append((min(slot + lag_here, SLOTS - 1), name, arg, whose, part))
    return sorted(out, key=lambda x: x[0])


PIECES = pieces()


def check_schedule():
    fills = [x for x in PIECES if x[4]]
    for first, again in zip(fills, fills[2:]):
        name, arg = first[1:3]
        engine = "dve" if name in ("out_proj", "down_proj", "up_proj") else "act"
        slot = next(x[0] for x in parts(engine) if x[1:3] == (name, arg) and x[4] == "")
        assert again[0] >= slot - (RING if engine == "act" else 0), (first, again)


PER_ITERATION = sum(x[4] for x in PIECES)
FILLS = {row: [x for x in PIECES if x[3] == row] for row in (TAIL, HERE, NEXT)}
N_TAIL = sum(x[4] for x in FILLS[TAIL])
N_NEXT = sum(x[4] for x in FILLS[NEXT])
assert PER_ITERATION % 2 == 0


class Row:

    def __init__(self, number, i=None, step=0):
        self.number, self.i, self.step = number, i, step
        self.parity = number % 2

    def __add__(self, n):
        return Row(self.number + n, self.i, self.step)

    def count(self, per, more):
        fixed = per * self.number + more
        if self.i is None:
            return fixed if fixed > 0 else None
        return self.i * (per * self.step) + fixed

    def last(self):
        return self.i is None and self.number == BATCH - 1

    def index(self):
        return self.number if self.i is None else self.i * self.step + self.number


def fill_number(row, name, arg):
    for at, x in enumerate(PIECES):
        if x[1:3] == (name, arg):
            break
    whose = x[3]
    before = sum(y[4] for y in PIECES[:at])
    it = row + (-whose)
    if it.i is None and it.number == -1:
        before = sum(y[4] for y in PIECES[:at] if y[3] == NEXT)
        return 0, before
    if it.i is None and it.number == 0:
        return 0, N_NEXT + sum(y[4] for y in PIECES[:at] if y[3] != TAIL)
    if it.i is None and it.number == BATCH:
        before = sum(y[4] for y in PIECES[:at] if y[3] == TAIL)
        return 0, N_NEXT + PER_ITERATION * BATCH - N_TAIL - N_NEXT + before
    if it.i is None and it.number == BATCH - 1:
        before = sum(y[4] for y in PIECES[:at] if y[3] != NEXT)
        return 0, N_NEXT + PER_ITERATION * it.number - N_TAIL + before
    return PER_ITERATION, N_NEXT - N_TAIL + before, it


class Fill:

    def __init__(self, row, name, arg):
        got = fill_number(row, name, arg)
        self.it = got[2] if len(got) == 3 else Row(0)
        self.per, self.more = got[0], got[1]
        number = self.more + self.per * self.it.number
        self.bank = number % 2

    def order(self):
        return self.per * self.it.number + self.more

    def filled(self):
        return self.it.count(self.per, self.more + 1)

    def emptied(self, after=1):
        fixed = self.more + self.per * self.it.number
        half = (fixed - self.bank) // 2 + after
        if self.it.i is None or self.per == 0:
            return half if half > 0 else None
        return self.it.i * (self.per * self.it.step // 2) + half


def wait(eng, semaphore, value):
    if value is not None:
        eng.wait_ge(semaphore, value)


def walk(eng, engine, unit, piece, drain):
    mine = parts(engine)

    def iteration(row, tail, following):
        for slot in range(SLOTS):
            unit(row, slot)
            for _, name, arg, whose, part in (x for x in mine if x[0] == slot):
                if (whose != TAIL or tail) and (whose != NEXT or following):
                    piece(row + whose, name, arg, part)
        drain(row)

    for _, name, arg, whose, part in mine:
        if whose == NEXT:
            piece(Row(0), name, arg, part)
    iteration(Row(0), False, True)
    with eng.Fori(0, (BATCH - 2) // 2) as i:
        iteration(Row(1, i, 2), True, True)
        iteration(Row(2, i, 2), True, True)
    iteration(Row(BATCH - 1), True, False)
    for _, name, arg, whose, part in mine:
        if whose == TAIL:
            piece(Row(BATCH - 1), name, arg, part)


def build(nc, a, out):
    check_schedule()
    ctx = ExitStack()
    with ctx:
        def sb(name, shape, dt=F32):
            return ctx.enter_context(nc.sbuf_tensor(name, shape, dt))

        def sem(name):
            return ctx.enter_context(nc.semaphore(name))

        decay = ctx.enter_context(nc.psum_tensor("decay", [P, RING, L], F32))
        h_t = ctx.enter_context(nc.psum_tensor("h_t", [P, 2, D_INNER], F32))
        banks = ctx.enter_context(nc.psum_tensor("banks", [P, 2, 512], F32))

        w_in = sb("w_in", [P, K_MODEL, 2 * D_INNER])
        w_conv = sb("w_conv", [P, 2, J, D_CONV])
        b_conv = sb("b_conv", [P, 2, J])
        conv_diag = sb("conv_diag", [P, 2, J, D_CONV, P])
        w_skip = sb("w_skip", [P, 2, J])
        skip_diag = sb("skip_diag", [P, 2, J, P])
        w_xproj = sb("w_xproj", [P, 2, J, PROJ])
        w_dt = sb("w_dt", [PROJ + 1, 2, D_INNER])
        a_neg = sb("a_neg", [P, 2, J, N_STATE])
        w_out = sb("w_out", [P, J, D_MODEL])
        w_gate = sb("w_gate", [P, K_MODEL, HIDDEN])
        w_up = sb("w_up", [P, K_MODEL, HIDDEN])
        w_down = sb("w_down", [P, H, D_MODEL])
        ident = sb("ident", [P, P])
        eps = sb("eps", [P, 1])
        marker = sb("marker", [P, 1])

        x = sb("x", [P, T, D_MODEL])
        x1 = sb("x1", [P, T, D_MODEL])
        normed = sb("normed", [P, T, D_MODEL])
        normed_t = sb("normed_t", [P, K_MODEL, L])
        stats = sb("stats", [P, T, 6])
        mean_vars = {k: sb(f"mean_var_{k}", [P, T, 2]) for k in LAYERNORMS}
        log_vars = {k: sb(f"log_var_{k}", [P, T]) for k in LAYERNORMS}
        rstds = {k: sb(f"rstd_{k}", [P, T]) for k in LAYERNORMS}
        x_in = sb("x_in", [P, 2, L + 2 * PAD])
        xc = sb("xc", [P, 2, J, L])
        proj = sb("proj", [PROJ + 1, 2, L])
        c_nat = sb("c_nat", [P, 2, 2, T, N_STATE])
        sp_e = sb("sp_e", [P, L])
        sp_log = sb("sp_log", [P, L])
        sp_w = sb("sp_w", [P, L])
        sp_relu = sb("sp_relu", [P, L])
        dt = sb("dt", [P, 2, J, L])
        dtx = sb("dtx", [P, 2, J, L])
        b_wide = sb("b_wide", [P, RING, L])
        drive = sb("drive", [P, RING, L])
        h = sb("h", [P, 2, J, L])
        acc = sb("acc", [P, 2, T, D_INNER])
        z = sb("z", [P, T, D_INNER])
        hidden = sb("hidden", [P, H, L])
        gated_t = hidden[:, 0:J, :]
        gate_i32 = acc[:, :, :, :].rearrange("p a t d -> p (a t d)")[:, 0:K_MODEL * HIDDEN].bitcast(I32)
        up_i32 = acc[:, :, :, :].rearrange("p a t d -> p (a t d)")[:, K_MODEL * HIDDEN:2 * K_MODEL * HIDDEN].bitcast(I32)
        down_i32 = hidden[:, :, :].rearrange("p a b -> p (a b)")[:, 0:H * D_MODEL].bitcast(I32)
        b_rows = nc.dram_tensor("b_rows", (2, 2, N_STATE, L), F32, kind="Internal").ap()

        w_in_loaded, w_conv_loaded, w_rest_loaded, w_int_loaded = map(sem, ("w_in_loaded", "w_conv_loaded", "w_rest_loaded", "w_int_loaded"))
        ident_zeroed, ident_made, consts_made = map(sem, ("ident_zeroed", "ident_made", "consts_made"))
        rows_made, diag_made = map(sem, ("rows_made", "diag_made"))
        a_min, a_exp, a_made, int_cast = map(sem, ("a_min", "a_exp", "a_made", "int_cast"))
        x_loaded, x1_loaded, out_stored = map(sem, ("x_loaded", "x1_loaded", "out_stored"))
        decay_made, drive_made, scan_made = map(sem, ("decay_made", "drive_made", "scan_made"))
        reset_made = sem("reset_made")
        h_t_made, acc_made = map(sem, ("h_t_made", "acc_made"))
        b_wide_loaded = [sem(f"b_wide_loaded{k}") for k in range(RING)]
        b_stored = [sem(f"b_stored{r}") for r in range(2)]
        bank_filled = sem("bank_filled")
        bank_emptied = [sem(f"bank_emptied{k}") for k in range(2)]
        correction_made, exp_made, log_made, one_plus_made = map(sem, ("correction_made", "exp_made", "log_made", "one_plus_made"))
        dt_made, dtx_made = map(sem, ("dt_made", "dtx_made"))
        gated = sem("gated")
        sig_made = sem("sig_made")
        ln = {k: {e: sem(f"ln_{k}_{e}") for e in ("stats", "mean", "log", "rstd", "normed", "added")} for k in LAYERNORMS}

        BANK = lambda f: banks[:, f.bank, :]

        def emptied(eng, row, *needs, free=None):
            for k in range(2):
                uses = [f for f in (Fill(row, name, arg) for name, arg in needs) if f.bank == k]
                if free is not None and free.bank == k:
                    wait(eng, bank_emptied[k], free.emptied(after=0))
                elif uses:
                    eng.wait_ge(bank_emptied[k], max(uses, key=Fill.order).emptied())

        block = ctx.enter_context(nc.Block())

        @block.sync
        def _(sp):
            def load_x(row):
                number = row.index()
                wait(sp, ln["in"]["normed"], row.count(1, 0))
                sp.dma_start(x[:, :, :], a["u"][bass.ds(number, 1)].rearrange("b (t p) d -> p (b t) d", p=P)).then_inc(x_loaded, 16)

            def load_x1(row):
                number = row.index()
                wait(sp, out_stored, row.count(32, 0))
                sp.dma_start(x1[:, :, :], a["u"][bass.ds(number, 1)].rearrange("b (t p) d -> p (b t) d", p=P)).then_inc(x1_loaded, 16)

            def load_b(row, step):
                r, n = divmod(step, N_STATE)
                if n == 0 and row.i is None:
                    sp.wait_ge(b_stored[r], row.count(16, 16))
                wait(sp, drive_made, row.count(SLOTS, J * (step - RING + 1)))
                sp.dma_start(b_wide[:, step % RING, :], b_rows[row.parity, r, n:n + 1, :].partition_broadcast(P)
                             ).then_inc(b_wide_loaded[step % RING], 16)

            sp.dma_start(x[:, :, :], a["u"][0:1].rearrange("b (t p) d -> p (b t) d", p=P)).then_inc(x_loaded, 16)
            sp.dma_start(w_in[:, :, :], a["in_proj_w"].rearrange("(k p) n -> p k n", p=P)).then_inc(w_in_loaded, 16)
            for r, d in enumerate(("fwd", "bwd")):
                sp.dma_start(w_xproj[:, r, :, :], a[f"{d}_x_proj_w"].rearrange("(j p) n -> p j n", p=P)).then_inc(w_rest_loaded, 16)
                sp.dma_start(w_dt[0:DT_RANK, r, :], a[f"{d}_dt_w"]).then_inc(w_rest_loaded, 16)
                sp.dma_start(w_dt[BIAS_ROW:BIAS_ROW + 1, r, :], a[f"{d}_dt_b"].rearrange("(o n) -> o n", o=1)).then_inc(w_rest_loaded, 16)
            sp.dma_start(w_out[:, :, :], a["out_proj_w"].rearrange("(j p) n -> p j n", p=P)).then_inc(w_rest_loaded, 16)

            def unit(row, slot):
                step, j = divmod(slot, J)
                if j == 0 and step == 0:
                    load_b(row, 0)
                    load_b(row, 1)
                    load_b(row, 2)
                if j == 0 and step + 3 < STEPS:
                    load_b(row, step + 3)

            def piece(row, name, arg, part):
                if name == "x_proj":
                    emptied(sp, row, ("x_proj", arg))
                    for k in range(RING):
                        wait(sp, b_wide_loaded[k], row.count(16 * STEPS // RING, -16 * STEPS // RING))
                    sp.dma_start(b_rows[row.parity, arg], proj[DT_RANK:DT_RANK + N_STATE, arg, :]).then_inc(b_stored[arg], 16)
                if name == "gate":
                    load_x1(row)
                if name == "z" and arg == 0 and not row.last():
                    load_x(row + 1)
                if name == "down_proj":
                    number = row.index()
                    sp.wait_ge(ln["ffn"]["added"], row.count(2, arg + 1))
                    sp.dma_start(out[bass.ds(number, 1), arg * 2 * P:(arg + 1) * 2 * P, :].rearrange("b (t p) d -> p (b t) d", p=P),
                                 x1[:, 2 * arg:2 * arg + 2, :]).then_inc(out_stored, 16)

            walk(sp, "sp", unit, piece, lambda row: None)
            sp.wait_ge(out_stored, 32 * BATCH)

        @block.gpsimd
        def _(pool):
            pool.memset(ident[:, :], 0.0).then_inc(ident_zeroed, 1)
            pool.wait_ge(ident_zeroed, 1)
            pool.affine_select(out=ident[:, :], in_=ident[:, :], compare_op=ALU.not_equal, fill=1.0, base=0,
                               pattern=[[-1, P]], channel_multiplier=1).then_inc(ident_made, 1)
            pool.memset(eps[:, :], LN_EPS)
            pool.memset(x_in[:, :, 0:PAD], 0.0)
            pool.memset(x_in[:, :, L + PAD:L + 2 * PAD], 0.0).then_inc(consts_made, 1)

            def unit(row, slot):
                step, j = divmod(slot, J)
                r = step // N_STATE
                if slot == SLOTS - RING * J and not row.last():
                    for k in range(2):
                        pool.wait_ge(b_stored[k], (row + 1).count(16, 16))
                if j == 0:
                    pool.wait_ge(b_wide_loaded[step % RING], row.count(16 * STEPS // RING, 16 * (step // RING + 1)))
                if step % N_STATE == 0:
                    pool.wait_ge(dtx_made, row.count(2 * J, J * r + j + 1))
                wait(pool, scan_made, row.count(SLOTS, slot + 1 - RING))
                pool.tensor_tensor(drive[:, slot % RING, :], dtx[:, r, j, :], b_wide[:, step % RING, :], ALU.mult).then_inc(drive_made, 1)

            def piece(row, name, arg, part):
                if name not in ("dt_fwd", "dt_bwd"):
                    return
                r = int(name == "dt_bwd")
                made = row.count(2 * J, J * r + arg + 1)
                pool.wait_ge(correction_made, made)
                wait(pool, decay_made, row.count(SLOTS, -SLOTS + SLOTS // 2 * (r + 1) - J + arg + 1))
                pool.tensor_tensor(dt[:, r, arg, :], sp_log[:, :], sp_w[:, :], ALU.subtract).then_inc(dt_made, 1)
                wait(pool, drive_made, row.count(SLOTS, -SLOTS + SLOTS // 2 * (r + 1) - J + arg + 1))
                pool.wait_ge(dt_made, made)
                pool.tensor_tensor(dtx[:, r, arg, :], dt[:, r, arg, :], xc[:, r, arg, :], ALU.mult).then_inc(dtx_made, 1)

            walk(pool, "pool", unit, piece, lambda row: None)

        @block.scalar
        def _(act):
            for r, d in enumerate(("fwd", "bwd")):
                act.dma_start(w_conv[:, r, :, :], a[f"{d}_conv_w"]).then_inc(w_conv_loaded, 16)
                act.dma_start(b_conv[:, r, :], a[f"{d}_conv_b"]).then_inc(w_conv_loaded, 16)
                act.dma_start(w_skip[:, r, :], a[f"{d}_D"]).then_inc(w_conv_loaded, 16)
                act.dma_start(a_neg[:, r, :, :], a[f"{d}_A_log"].rearrange("(j p) n -> p j n", p=P)).then_inc(w_conv_loaded, 16)
            act.dma_start(gate_i32.rearrange("p (k n) -> p k n", k=K_MODEL), a["w_gate"].rearrange("(k p) n -> p k n", p=P)).then_inc(w_int_loaded, 16)
            act.dma_start(up_i32.rearrange("p (k n) -> p k n", k=K_MODEL), a["w_up"].rearrange("(k p) n -> p k n", p=P)).then_inc(w_int_loaded, 16)
            act.dma_start(down_i32.rearrange("p (i n) -> p i n", i=H), a["w_down"].rearrange("(i p) n -> p i n", p=P)).then_inc(w_int_loaded, 16)
            act.wait_ge(consts_made, 1)
            act.preload_act_table_set("natural_log_exp_and_others")
            act.wait_ge(a_min, 1)
            act.activation(a_neg[:, :, :, :], a_neg[:, :, :, :], ACT.Exp).then_inc(a_exp, 1)

            table = ["exp"]

            def use_table(which):
                if which == "exp" and table[0] != "exp":
                    act.preload_act_table_set("natural_log_exp_and_others")
                table[0] = which

            def unit(row, slot):
                use_table("exp")
                step, j = divmod(slot, J)
                r, n = divmod(step, N_STATE)
                if n == 0:
                    act.wait_ge(dt_made, row.count(2 * J, J * r + j + 1))
                if slot == 0 and row.i is None and row.number == 0:
                    act.wait_ge(a_made, 1)
                wait(act, scan_made, row.count(SLOTS, slot + 1 - RING))
                lo = 1 - r
                act.activation(decay[:, slot % RING, lo:lo + L - 1], dt[:, r, j, lo:lo + L - 1], ACT.Exp,
                               scale=a_neg[:, r, j, n:n + 1]).then_inc(decay_made, 1)

            def read_bank(row, name, arg):
                f = Fill(row, name, arg)
                act.wait_ge(bank_filled, f.filled())
                return f, bank_emptied[f.bank]

            def rstd_of(kind, count, tiles):
                use_table("exp")
                act.wait_ge(ln[kind]["mean"], count)
                act.activation(log_vars[kind][:, tiles], mean_vars[kind][:, tiles, 1], ACT.Ln, bias=eps[:, 0:1]).then_inc(ln[kind]["log"], 1)
                act.wait_ge(ln[kind]["log"], count)
                act.activation(rstds[kind][:, tiles], log_vars[kind][:, tiles], ACT.Exp, scale=-0.5).then_inc(ln[kind]["rstd"], 1)

            def piece(row, name, arg, part):
                if name in ("norm_in", "norm_x1"):
                    rstd_of(name[5:], row.count(1, 1), slice(0, T))
                elif name in ("out_proj", "down_proj"):
                    rstd_of("attn" if name == "out_proj" else "ffn", row.count(2, arg + 1), slice(2 * arg, 2 * arg + 2))
                elif name in ("x_t", "x1_t"):
                    f, done = read_bank(row, name, arg)
                    act.activation(normed_t[:, arg, :], BANK(f), ACT.Copy).then_inc(done, 1)
                elif name == "in_proj":
                    f, done = read_bank(row, name, arg)
                    act.activation(x_in[:, arg % 2, PAD:PAD + L], BANK(f), ACT.Copy).then_inc(done, 1)
                elif name in ("conv_fwd", "conv_bwd"):
                    r = int(name == "conv_bwd")
                    use_table("silu")
                    wait(act, dtx_made, row.count(2 * J, -J + J * r))
                    f, done = read_bank(row, name, arg)
                    act.activation(xc[:, r, arg, :], BANK(f), ACT.Silu, bias=b_conv[:, r, arg:arg + 1]).then_inc(done, 1)
                elif name == "x_proj":
                    wait(act, b_stored[arg], row.count(16, 0))
                    f, done = read_bank(row, name, arg)
                    act.activation(proj[0:PROJ, arg, :], banks[0:PROJ, f.bank, :], ACT.Copy).then_inc(done, 1)
                elif name == "c_t":
                    wait(act, acc_made, row.count(SLOTS, -SLOTS))
                    f, done = read_bank(row, name, arg)
                    act.activation(c_nat[:, row.parity, arg, :, :],
                                   banks[:, f.bank, 0:T * PROJ].rearrange("p (t c) -> p t c", t=T)[:, :, DT_RANK + N_STATE:PROJ],
                                   ACT.Copy).then_inc(done, 1)
                elif name == "d_term":
                    if row.i is None and row.number == 0:
                        act.wait_ge(int_cast, 1)
                    f, done = read_bank(row, name, arg)
                    act.activation(acc[:, row.parity, arg, :], BANK(f), ACT.Copy).then_inc(done, 1)
                elif name in ("dt_fwd", "dt_bwd"):
                    r = int(name == "dt_bwd")
                    made = row.count(2 * J, J * r + arg + 1)
                    use_table("exp")
                    wait(act, dt_made, row.count(2 * J, J * r + arg))
                    f, done = read_bank(row, name, arg)
                    act.activation(sp_relu[:, :], BANK(f), ACT.Relu)
                    act.activation(sp_e[:, :], BANK(f), ACT.Abs).then_inc(done, 1)
                    act.wait_ge(done, f.emptied())
                    act.activation(sp_e[:, :], sp_e[:, :], ACT.Exp, scale=-1.0).then_inc(exp_made, 1)
                    act.wait_ge(exp_made, made)
                    act.activation(sp_w[:, :], sp_e[:, :], ACT.Copy, bias=1.0).then_inc(one_plus_made, 1)
                    act.activation(sp_log[:, :], sp_e[:, :], ACT.Ln, bias=1.0).then_inc(log_made, 1)
                elif name == "z":
                    wait(act, gated, row.count(T, 0))
                    use_table("silu")
                    f, done = read_bank(row, name, arg)
                    act.activation(z[:, arg, :], BANK(f), ACT.Silu).then_inc(done, 1)
                elif name == "gated_t":
                    f, done = read_bank(row, name, arg)
                    act.activation(gated_t[:, arg, :], BANK(f), ACT.Copy).then_inc(done, 1)
                elif name == "gate_proj":
                    use_table("silu")
                    f, done = read_bank(row, name, arg)
                    act.activation(hidden[:, arg, :], BANK(f), ACT.Silu, scale=SCALE).then_inc(done, 1)

            walk(act, "act", unit, piece, lambda row: None)

        @block.tensor
        def _(pe):
            def fill_bank(row, name, arg, *needs):
                f = Fill(row, name, arg)
                emptied(pe, row, *needs, free=f)
                return f

            def transpose_step(row, step, t):
                number = J * step + t
                pe.wait_ge(scan_made, row.count(SLOTS, J * step + J))
                wait(pe, acc_made, row.count(SLOTS, number + 1 - 2))
                for j in range(J):
                    last = pe.transpose(h_t[:, number % 2, j * P:(j + 1) * P], h[:, step % 2, j, t * P:(t + 1) * P], ident[:, :])
                last.then_inc(h_t_made, 1)

            def unit(row, slot):
                step, j = divmod(slot, J)
                if step:
                    transpose_step(row, step - 1, j)

            def drain(row):
                for t in range(T):
                    transpose_step(row, STEPS - 1, t)

            pe.wait_ge(ident_made, 1)
            pe.wait_ge(consts_made, 1)
            pe.wait_ge(rows_made, 1)
            pe.wait_ge(w_in_loaded, 16)

            def piece(row, name, arg, part):
                if name in ("x_t", "x1_t"):
                    pe.wait_ge(ln["in" if name == "x_t" else "x1"]["normed"], row.count(1, 1))
                    f = fill_bank(row, name, arg)
                    for t in range(T):
                        last = pe.transpose(banks[:, f.bank, t * P:(t + 1) * P], normed[:, t, arg * P:(arg + 1) * P], ident[:, :])
                elif name == "in_proj":
                    f = fill_bank(row, name, arg, *[("x_t", k) for k in range(K_MODEL)])
                    for k in range(K_MODEL):
                        last = pe.matmul(BANK(f), w_in[:, k, arg * P:(arg + 1) * P], normed_t[:, k, :], start=(k == 0), stop=(k == K_MODEL - 1))
                elif name in ("conv_fwd", "conv_bwd"):
                    r = int(name == "conv_bwd")
                    if row.i is None and row.number == 0 and arg == 0:
                        pe.wait_ge(diag_made, 1)
                    f = fill_bank(row, name, arg, ("in_proj", arg))
                    for tap in range(D_CONV):
                        at = tap if r == 0 else 2 * PAD - tap
                        last = pe.matmul(BANK(f), conv_diag[:, r, arg, tap, :], x_in[:, arg % 2, at:at + L],
                                         start=(tap == 0), stop=(tap == D_CONV - 1))
                elif name == "x_proj":
                    if row.i is None and row.number == 0:
                        pe.wait_ge(w_rest_loaded, 16 * 7)
                    f = fill_bank(row, name, arg, *[("conv_bwd" if arg else "conv_fwd", j) for j in range(J)])
                    for j in range(J):
                        last = pe.matmul(banks[0:PROJ, f.bank, :], w_xproj[:, arg, j, :], xc[:, arg, j, :], start=(j == 0), stop=(j == J - 1))
                elif name == "c_t":
                    f = fill_bank(row, name, arg, ("x_proj", arg))
                    for t in range(T):
                        last = pe.transpose(banks[:, f.bank, t * PROJ:(t + 1) * PROJ], proj[0:PROJ, arg, t * P:(t + 1) * P], ident[0:PROJ, 0:PROJ])
                elif name in ("dt_fwd", "dt_bwd"):
                    r = int(name == "dt_bwd")
                    f = fill_bank(row, name, arg, ("x_proj", r))
                    last = pe.matmul(BANK(f), w_dt[:, r, arg * P:(arg + 1) * P], proj[:, r, :], start=True, stop=True)
                elif name == "d_term":
                    f = fill_bank(row, name, arg, *[("conv_bwd", j) for j in range(J)])
                    for j in range(J):
                        for r in range(2):
                            last = pe.matmul(banks[:, f.bank, j * P:(j + 1) * P], xc[:, r, j, arg * P:(arg + 1) * P], skip_diag[:, r, j, :],
                                             start=(r == 0), stop=(r == 1))
                elif name == "z":
                    f = fill_bank(row, name, arg)
                    for k in range(K_MODEL):
                        last = pe.matmul(BANK(f), normed_t[:, k, arg * P:(arg + 1) * P], w_in[:, k, D_INNER:2 * D_INNER],
                                         start=(k == 0), stop=(k == K_MODEL - 1))
                elif name == "gated_t":
                    pe.wait_ge(gated, row.count(T, T))
                    f = fill_bank(row, name, arg)
                    for t in range(T):
                        last = pe.transpose(banks[:, f.bank, t * P:(t + 1) * P], acc[:, row.parity, t, arg * P:(arg + 1) * P], ident[:, :])
                elif name == "out_proj":
                    f = fill_bank(row, name, arg, *[("gated_t", k) for k in range(J)])
                    for t in (2 * arg, 2 * arg + 1):
                        for k in range(J):
                            last = pe.matmul(banks[:, f.bank, (t % 2) * D_MODEL:(t % 2 + 1) * D_MODEL], gated_t[:, k, t * P:(t + 1) * P],
                                             w_out[:, k, :], start=(k == 0), stop=(k == J - 1))
                elif name in ("gate_proj", "up_proj"):
                    f = fill_bank(row, name, arg, *[("x1_t", k) for k in range(K_MODEL)])
                    w = w_gate if name == "gate_proj" else w_up
                    for k in range(K_MODEL):
                        last = pe.matmul(BANK(f), w[:, k, arg * P:(arg + 1) * P], normed_t[:, k, :], start=(k == 0), stop=(k == K_MODEL - 1))
                elif name == "down_proj":
                    f = fill_bank(row, name, arg, *[("up_proj", i) for i in range(H)])
                    for t in (2 * arg, 2 * arg + 1):
                        for i in range(H):
                            last = pe.matmul(banks[:, f.bank, (t % 2) * D_MODEL:(t % 2 + 1) * D_MODEL], hidden[:, i, t * P:(t + 1) * P],
                                             w_down[:, i, :], start=(i == 0), stop=(i == H - 1))
                else:
                    return
                last.then_inc(bank_filled, 1)

            walk(pe, "pe", unit, piece, drain)

        @block.vector
        def _(dve):
            dve.memset(proj[BIAS_ROW:BIAS_ROW + 1, :, :], 1.0)
            dve.memset(w_dt[DT_RANK:PROJ, :, :], 0.0).then_inc(rows_made, 1)
            dve.wait_ge(w_conv_loaded, 16 * 8)
            dve.tensor_scalar(a_neg[:, :, :, :], a_neg[:, :, :, :], A_LOG_MAX, None, ALU.min).then_inc(a_min, 1)

            def weights():
                dve.wait_ge(ident_made, 1)
                for j in range(J):
                    for r in range(2):
                        for tap in range(D_CONV):
                            dve.tensor_scalar(conv_diag[:, r, j, tap, :], ident[:, :], w_conv[:, r, j, tap:tap + 1], None, ALU.mult)
                        last = dve.tensor_scalar(skip_diag[:, r, j, :], ident[:, :], w_skip[:, r, j:j + 1], None, ALU.mult)
                last.then_inc(diag_made, 1)
                dve.wait_ge(a_exp, 1)
                dve.tensor_scalar(a_neg[:, :, :, :], a_neg[:, :, :, :], -1.0, None, ALU.mult).then_inc(a_made, 1)
                dve.wait_ge(w_int_loaded, 16 * 3)
                flat = lambda w: w[:, :, :].rearrange("p a b -> p (a b)")
                dve.tensor_copy(flat(w_gate), gate_i32)
                dve.tensor_copy(flat(w_up), up_i32)
                dve.tensor_copy(flat(w_down), down_i32).then_inc(int_cast, 1)

            def scan(row, slot):
                step, j = divmod(slot, J)
                r, n = divmod(step, N_STATE)
                bank = slot % RING
                dve.wait_ge(decay_made, row.count(SLOTS, slot + 1))
                if n == 0:
                    first = 0 if r == 0 else L - 1
                    dve.memset(decay[:, bank, first:first + 1], 0.0).then_inc(reset_made, 1)
                    dve.wait_ge(reset_made, row.count(2 * J, J * r + j + 1))
                dve.wait_ge(drive_made, row.count(SLOTS, slot + 1))
                wait(dve, h_t_made, row.count(SLOTS, J * (step - 1)))
                order = slice(0, L) if r == 0 else slice(L - 1, None, -1)
                dve.tensor_tensor_scan(h[:, step % 2, j, order], decay[:, bank, order], drive[:, bank, order], 0.0,
                                       ALU.mult, ALU.add).then_inc(scan_made, 1)

            def accumulate(row, step, t):
                r, n = divmod(step, N_STATE)
                number = J * step + t
                if n == 0:
                    emptied(dve, row, ("c_t", r), *([("d_term", t)] if step == 0 else []))
                dve.wait_ge(h_t_made, row.count(SLOTS, number + 1))
                if step:
                    dve.wait_ge(acc_made, row.count(SLOTS, number + 1 - T))
                dve.scalar_tensor_tensor(out=acc[:, row.parity, t, :], in0=h_t[:, number % 2, :], scalar=c_nat[:, row.parity, r, t, n:n + 1],
                                         in1=acc[:, row.parity, t, :], op0=ALU.mult, op1=ALU.add).then_inc(acc_made, 1)

            def unit(row, slot):
                step, j = divmod(slot, J)
                scan(row, slot)
                if step:
                    accumulate(row, step - 1, j)

            def drain(row):
                for t in range(T):
                    accumulate(row, STEPS - 1, t)

            def moments(kind, count, src, tiles):
                for k, t in enumerate(tiles):
                    last = dve.bn_stats(stats[:, t, :], src(k))
                last.then_inc(ln[kind]["stats"], 1)
                dve.wait_ge(ln[kind]["stats"], count)
                dve.memset(marker[:, :], 0.0)
                for t in tiles:
                    last = dve.bn_aggr(mean_vars[kind][:, t, :], stats[:, t, :])
                last.then_inc(ln[kind]["mean"], 1)

            def normalise(kind, count, src, tiles):
                dve.wait_ge(ln[kind]["rstd"], count)
                for k, t in enumerate(tiles):
                    last = dve.tensor_scalar(normed[:, t, :], src(k), mean_vars[kind][:, t, 0:1], rstds[kind][:, t:t + 1], ALU.subtract, ALU.mult)
                return last

            def piece(row, name, arg, part):
                if name == "norm_in":
                    if part == "stats":
                        dve.wait_ge(x_loaded, row.count(16, 16))
                        moments("in", row.count(1, 1), lambda t: x[:, t, :], range(T))
                        return
                    wait(dve, ln["ffn"]["added"], row.count(2, -2))
                    normalise("in", row.count(1, 1), lambda t: x[:, t, :], range(T)).then_inc(ln["in"]["normed"], 1)
                    if row.i is None and row.number == 0:
                        weights()
                elif name == "d_term":
                    pass
                elif name in ("dt_fwd", "dt_bwd"):
                    r = int(name == "dt_bwd")
                    made = row.count(2 * J, J * r + arg + 1)
                    dve.wait_ge(one_plus_made, made)
                    dve.wait_ge(log_made, made)
                    dve.scalar_tensor_tensor(out=sp_w[:, :], in0=sp_w[:, :], scalar=1.0, in1=sp_e[:, :], op0=ALU.subtract, op1=ALU.subtract)
                    dve.tensor_tensor(sp_log[:, :], sp_log[:, :], sp_relu[:, :], ALU.add).then_inc(correction_made, 1)
                elif name == "gate":
                    emptied(dve, row, *[("z", t) for t in range(T)])
                    dve.wait_ge(acc_made, row.count(SLOTS, SLOTS))
                    for t in range(T):
                        dve.tensor_tensor(acc[:, row.parity, t, :], acc[:, row.parity, t, :], z[:, t, :], ALU.mult).then_inc(gated, 1)
                elif name in ("out_proj", "down_proj"):
                    kind = "attn" if name == "out_proj" else "ffn"
                    count = row.count(2, arg + 1)
                    tiles = range(2 * arg, 2 * arg + 2)
                    f = Fill(row, name, arg)
                    rows = lambda k: banks[:, f.bank, k * D_MODEL:(k + 1) * D_MODEL]
                    if part == "stats":
                        dve.wait_ge(bank_filled, f.filled())
                        moments(kind, count, rows, tiles)
                        return
                    normalise(kind, count, rows, tiles).then_inc(bank_emptied[f.bank], 1)
                    dve.wait_ge(bank_emptied[f.bank], f.emptied())
                    if name == "out_proj":
                        dve.wait_ge(x1_loaded, row.count(16, 16))
                    dve.tensor_tensor(x1[:, 2 * arg:2 * arg + 2, :], x1[:, 2 * arg:2 * arg + 2, :], normed[:, 2 * arg:2 * arg + 2, :], ALU.add
                                      ).then_inc(ln[kind]["added"], 1)
                elif name == "norm_x1":
                    if part == "stats":
                        dve.wait_ge(ln["attn"]["added"], row.count(2, 2))
                        moments("x1", row.count(1, 1), lambda t: x1[:, t, :], range(T))
                        return
                    normalise("x1", row.count(1, 1), lambda t: x1[:, t, :], range(T)).then_inc(ln["x1"]["normed"], 1)
                elif name == "up_proj":
                    f = Fill(row, name, arg)
                    dve.wait_ge(bank_filled, f.filled())
                    emptied(dve, row, ("gate_proj", arg))
                    dve.scalar_tensor_tensor(out=hidden[:, arg, :], in0=BANK(f), scalar=SCALE * SCALE, in1=hidden[:, arg, :],
                                             op0=ALU.mult, op1=ALU.mult).then_inc(bank_emptied[f.bank], 1)

            walk(dve, "dve", unit, piece, drain)


_NAMES = {
    "u": "L0_attn_u", "in_proj_w": "L0_attn_in_proj_w", "out_proj_w": "L0_attn_out_proj_w",
    "fwd_conv_w": "L0_attn_fwd_conv_w", "fwd_conv_b": "L0_attn_fwd_conv_b", "fwd_x_proj_w": "L0_attn_fwd_x_proj_w",
    "fwd_dt_w": "L0_attn_fwd_dt_w", "fwd_dt_b": "L0_attn_fwd_dt_b", "fwd_A_log": "L0_attn_fwd_A_log", "fwd_D": "L0_attn_fwd_D",
    "bwd_conv_w": "L0_attn_bwd_conv_w", "bwd_conv_b": "L0_attn_bwd_conv_b", "bwd_x_proj_w": "L0_attn_bwd_x_proj_w",
    "bwd_dt_w": "L0_attn_bwd_dt_w", "bwd_dt_b": "L0_attn_bwd_dt_b", "bwd_A_log": "L0_attn_bwd_A_log", "bwd_D": "L0_attn_bwd_D",
    "w_gate": "L0_ffn_w_gate", "w_up": "L0_ffn_w_up", "w_down": "L0_ffn_w_down",
}
_TRANSPOSED = ("in_proj_w", "out_proj_w", "fwd_x_proj_w", "bwd_x_proj_w", "fwd_dt_w", "bwd_dt_w", "w_gate", "w_up", "w_down")
_CHANNELS = ("fwd_conv_w", "fwd_conv_b", "fwd_D", "bwd_conv_w", "bwd_conv_b", "bwd_D")


def kernel(**inputs):
    import numpy as _np
    import concourse.bacc as _bacc
    from concourse import mybir as _mybir
    from concourse.bass_utils import run_bass_kernel_spmd as _run

    nc = _bacc.Bacc("TRN2", target_bir_lowering=False, num_devices=1)
    arrays, args = {}, {}
    for name, given in _NAMES.items():
        v = _np.asarray(inputs[given])
        if name in _TRANSPOSED:
            v = v.T
        elif name in _CHANNELS:
            v = _np.moveaxis(v.reshape(J, P, *[n for n in v.shape[1:] if n > 1]), 0, 1)
        v = _np.ascontiguousarray(v)
        arrays[f"in_{name}"] = v
        args[name] = nc.dram_tensor(f"in_{name}", v.shape, _mybir.dt.from_np(v.dtype), kind="ExternalInput").ap()
    out = nc.dram_tensor("out", (BATCH, L, D_MODEL), _mybir.dt.float32, kind="ExternalOutput").ap()
    build(nc, args, out)
    r = _run(nc, [arrays], core_ids=[0])
    return r.results[0]["out"]
```

```python
from contextlib import ExitStack

import concourse.bass as bass
from concourse import mybir

F32 = mybir.dt.float32
I32 = mybir.dt.int32
ALU = mybir.AluOpType
ACT = mybir.ActivationFunctionType

P = 128
BATCH, L, D_MODEL = 8, 512, 256
D_INNER, N_STATE, DT_RANK, D_CONV = 512, 16, 64, 4
HIDDEN = 768
J = D_INNER // P
K_MODEL = D_MODEL // P
T = L // P
H = HIDDEN // P
PROJ = DT_RANK + 2 * N_STATE
BIAS_ROW = PROJ
PAD = D_CONV - 1
STEPS = 2 * N_STATE
SLOTS = STEPS * J
RING = 4
PAIR_WORK = 2.0
CARRIED = 1.0
DT_GAP = 3
NORM_GAP = {"norm_x1": (2, 3), "norm_in": (4, 3)}
LN_EPS = 1e-5
SCALE = 1.0 / 127.0
A_LOG_MAX = 84.0

TAIL, HERE, NEXT = -1, 0, 1
WORK = {"dt_bwd": (1, 1), "dt_fwd": (1, 1), "gated_t": (.5, 1), "out_proj": (4, 4), "z": (2, 2), "x1_t": (.5, 1),
        "gate_proj": (2, 2), "up_proj": (2, 2), "down_proj": (6, 6), "x_t": (.5, 1), "in_proj": (2, 2),
        "conv_fwd": (4, 4), "conv_bwd": (4, 4), "x_proj": (4, 4), "c_t": (.5, 1), "d_term": (2, 2)}


def several(name, whose, args, first=0):
    return [(name, k, whose, first) for k in args]


START = (
    [("norm_in", 0, HERE, 0)] + several("x_t", HERE, range(K_MODEL))
    + several("in_proj", HERE, range(2)) + [("conv_fwd", 0, HERE, 0), ("in_proj", 2, HERE, 0), ("conv_fwd", 1, HERE, 0),
                                           ("in_proj", 3, HERE, 0), ("conv_fwd", 2, HERE, 0), ("conv_fwd", 3, HERE, 0)]
    + [("x_proj", 0, HERE, 0)] + [("dt_fwd", 0, HERE, 0), ("c_t", 0, HERE, 0)] + several("dt_fwd", HERE, range(1, J)))
FIRST_ONLY = (
    several("conv_bwd", HERE, range(J), 2) + [("x_proj", 1, HERE, 0), ("c_t", 1, HERE, 0)]
    + [x for k in (0, 2) for x in several("dt_bwd", HERE, [k]) + several("d_term", HERE, [k]) + several("z", HERE, [k, k + 1])
       + several("dt_bwd", HERE, [k + 1]) + several("d_term", HERE, [k + 1])])
LATER_ORDER = (
    several("d_term", HERE, [2, 3]) + several("gate", TAIL, [0], 3) + several("gated_t", TAIL, [1, 0, 2, 3], 5)
    + several("out_proj", TAIL, [0]) + several("x_proj", HERE, [1]) + several("z", HERE, [0, 1])
    + several("out_proj", TAIL, [1]) + several("norm_x1", TAIL, [0]) + several("z", HERE, [2, 3]) + several("c_t", HERE, [1])
    + several("x1_t", TAIL, [0, 1]) + several("gate_proj", TAIL, [0, 1]) + several("up_proj", TAIL, [0])
    + several("dt_bwd", HERE, [0]) + several("up_proj", TAIL, [1]) + several("norm_in", NEXT, [0])
    + several("dt_bwd", HERE, [1]) + several("gate_proj", TAIL, [2, 3]) + several("up_proj", TAIL, [2])
    + several("dt_bwd", HERE, [2]) + several("up_proj", TAIL, [3]) + several("gate_proj", TAIL, [4, 5])
    + several("dt_bwd", HERE, [3]) + several("up_proj", TAIL, [4, 5]) + several("x_t", NEXT, [0])
    + several("down_proj", TAIL, [0]) + several("x_t", NEXT, [1]) + several("down_proj", TAIL, [1])
    + several("in_proj", NEXT, [0, 1, 2, 3]) + several("conv_fwd", NEXT, [0, 1, 2, 3]) + several("x_proj", NEXT, [0])
    + several("dt_fwd", NEXT, [0]) + several("conv_bwd", NEXT, [0, 1]) + several("dt_fwd", NEXT, [1, 2])
    + several("conv_bwd", NEXT, [2]) + several("dt_fwd", NEXT, [3]) + several("conv_bwd", NEXT, [3])
    + several("d_term", NEXT, [0, 1]) + several("c_t", NEXT, [0]))

LAGS = {
    "sp": {"": (4, {"gate": 0, "z": 0, "down_proj": 6})},
    "act": {"": (4, {"conv_bwd": 2, "norm_x1": 2, "x_t": 2, "conv_fwd": 2, "z": 2})},
    "dve": {"stats": (0, {}), "": (2, {"gate": 0, "up_proj": 0, "dt_fwd": 4, "dt_bwd": 4})},
    "pool": {"sum": (6, {}), "dt": (8, {}), "": (10, {})},
}
PAIRED = {("z", k, HERE): ("z", k + 1, HERE) for k in range(0, T, 2)}
PAIRED |= {("conv_fwd", j, NEXT): ("conv_fwd", j + 1, NEXT) for j in range(0, J, 2)}
PAIRED |= {("conv_bwd", j, HERE): ("conv_bwd", j + 1, HERE) for j in range(0, J, 2)}
PAIRED |= {("gate_proj", i, TAIL): ("gate_proj", i + 1, TAIL) for i in range(0, H, 2)}
ON_VECTOR = ("out_proj", "down_proj", "up_proj")
LAYERNORMS = ("in", "attn", "x1", "ffn")
STATS = ("norm_in", "norm_x1", "out_proj", "down_proj")


def needs(name, arg):
    return {
        "in_proj": [("x_t", k) for k in range(K_MODEL)],
        "conv_fwd": [("in_proj", arg)], "conv_bwd": [("in_proj", arg)],
        "x_proj": [("conv_bwd" if arg else "conv_fwd", j) for j in range(J)],
        "c_t": [("x_proj", arg)], "dt_fwd": [("x_proj", 0)], "dt_bwd": [("x_proj", 1)],
        "d_term": [("conv_bwd", j) for j in range(J)],
        "out_proj": [("gated_t", k) for k in range(J)],
        "gate_proj": [("x1_t", k) for k in range(K_MODEL)],
        "down_proj": [("up_proj", i) for i in range(H)],
    }.get(name, [])


def place(order, on_vector):
    out, fills, slot_now, room, last_dt, ready = [], [], 1, PAIR_WORK, -DT_GAP, 0
    last = {}
    for name, arg, whose, first in order:
        if name not in WORK:
            slot = max(first, out[-1][0] + NORM_GAP[name][0] if name in NORM_GAP else 0)
            ready = slot + NORM_GAP.get(name, (0, 0))[1]
            last[name, arg, whose] = slot
            out.append((slot, name, arg, whose, 0))
            continue
        work, chunks = WORK[name]
        if name in ("x1_t", "x_t"):
            first = max(first, ready)
        if name in ("dt_fwd", "dt_bwd"):
            first = max(first, last_dt + DT_GAP)
        for use in fills[-2:-1] + [x for x in last if x[:2] in needs(name, arg) and x[2] == whose]:
            lag, by_name = LAGS["dve"][""] if use[0] in on_vector else (0, {})
            first = max(first, last[PAIRED.get(use, use)] + by_name.get(use[0], lag) + 1)
        for chunk in range(chunks):
            while first > slot_now or work / chunks > room:
                slot_now, room = slot_now + 2, PAIR_WORK + min(room, CARRIED)
            room -= work / chunks
            slot = slot_now
            out.append((slot, name, arg, whose, chunk))
        last[name, arg, whose] = slot
        fills.append((name, arg, whose))
        if name in ("dt_fwd", "dt_bwd"):
            last_dt = slot
    assert out[-1][0] < SLOTS, out[-1]
    lists = {"pe": sorted(out, key=lambda x: x[0])}
    for engine, lags in LAGS.items():
        mine = []
        for name, arg, whose in last:
            slot = last[PAIRED.get((name, arg, whose), (name, arg, whose)) if engine == "act" else (name, arg, whose)]
            for part, (lag, by_name) in lags.items():
                if part and name not in (STATS if part == "stats" else ("dt_fwd", "dt_bwd")):
                    continue
                mine.append((min((slot + by_name.get(name, lag)) // 2 * 2 + 1, SLOTS - 1), name, arg, whose, part))
        lists[engine] = sorted(mine, key=lambda x: x[0])
    return lists


def in_order(order):
    lists = {"pe": [(0, name, arg, whose, chunk) for name, arg, whose, _ in order for chunk in range(WORK.get(name, (0, 1))[1])]}
    for engine, lags in LAGS.items():
        lists[engine] = [(0, name, arg, whose, part) for name, arg, whose, _ in order for part in lags if not part or name in (STATS if part == "stats" else ("dt_fwd", "dt_bwd"))]
    return lists


STARTING = in_order(START)
FIRST = place(FIRST_ONLY + [x for x in LATER_ORDER if x[2] == NEXT], (*ON_VECTOR, "d_term"))
LATER = place(LATER_ORDER, ON_VECTOR)
ENDING = in_order([x for x in LATER_ORDER if x[2] == TAIL])


def fill_numbers():
    order = [(0, x) for x in STARTING["pe"]]
    for it in range(BATCH):
        order += [(it + x[3], x) for x in (LATER if it else FIRST)["pe"] if it + x[3] < BATCH]
    order += [(BATCH - 1, x) for x in ENDING["pe"]]
    fills = [(row, *x[1:3]) for row, x in order if x[1] in WORK and x[4] == 0]
    assert len(set(fills)) == len(fills)
    return {x: n for n, x in enumerate(fills)}


FILL_NUMBERS = fill_numbers()
PER_ITERATION = len([x for x in LATER["pe"] if x[1] in WORK and x[4] == 0])
assert PER_ITERATION % 2 == 0


class Row:

    def __init__(self, number, i=None, step=0):
        self.number, self.i, self.step = number, i, step
        self.parity = number % 2

    def __add__(self, n):
        return Row(self.number + n, self.i, self.step)

    def count(self, per, more):
        fixed = per * self.number + more
        assert self.i is None or fixed > 0
        if self.i is None:
            return fixed if fixed > 0 else None
        return self.i * (per * self.step) + fixed

    def first(self):
        return self.i is None and self.number == 0

    def last(self):
        return self.i is None and self.number == BATCH - 1

    def index(self):
        return self.number if self.i is None else self.i * self.step + self.number


class Fill:

    def __init__(self, row, name, arg):
        self.row = row
        self.number = FILL_NUMBERS[row.number, name, arg]
        self.bank = self.number % 2

    def later(self, per_iteration):
        return 0 if self.row.i is None else self.row.i * (per_iteration * self.row.step)

    def filled(self):
        return self.later(PER_ITERATION) + (self.number + 1)

    def emptied(self, after=1):
        half = self.number // 2 + after
        return self.later(PER_ITERATION // 2) + half if half > 0 else None


def wait(eng, semaphore, value):
    if value is not None:
        eng.wait_ge(semaphore, value)


def walk(eng, engine, unit, piece, drain):
    def iteration(row, lists, following):
        for slot in range(SLOTS):
            unit(row, slot)
            for _, name, arg, whose, part in (x for x in lists[engine] if x[0] == slot):
                if whose != NEXT or following:
                    piece(row + whose, name, arg, part)

    def pieces(row, lists):
        for _, name, arg, _, part in lists[engine]:
            piece(row, name, arg, part)

    pieces(Row(0), STARTING)
    iteration(Row(0), FIRST, True)
    with eng.Fori(0, (BATCH - 2) // 2) as i:
        iteration(Row(1, i, 2), LATER, True)
        iteration(Row(2, i, 2), LATER, True)
    iteration(Row(BATCH - 1), LATER, False)
    drain(Row(BATCH - 1))
    pieces(Row(BATCH - 1), ENDING)


def build(nc, a, out):
    ctx = ExitStack()
    with ctx:
        def sb(name, shape, dt=F32):
            return ctx.enter_context(nc.sbuf_tensor(name, shape, dt))

        def sem(name):
            return ctx.enter_context(nc.semaphore(name))

        decay = ctx.enter_context(nc.psum_tensor("decay", [P, RING, L], F32))
        h_t = ctx.enter_context(nc.psum_tensor("h_t", [P, 2, D_INNER], F32))
        banks = ctx.enter_context(nc.psum_tensor("banks", [P, 2, 512], F32))

        w_in = sb("w_in", [P, K_MODEL, 2 * D_INNER])
        w_conv = sb("w_conv", [P, 2, J, D_CONV])
        b_conv = sb("b_conv", [P, 2, J])
        conv_diag = sb("conv_diag", [P, 2, J, D_CONV, P])
        w_skip = sb("w_skip", [P, 2, J])
        skip_diag = sb("skip_diag", [P, 2, J, P])
        w_xproj = sb("w_xproj", [P, 2, J, PROJ])
        w_dt = sb("w_dt", [PROJ + 1, 2, D_INNER])
        a_neg = sb("a_neg", [P, 2, J, N_STATE])
        w_out = sb("w_out", [P, J, D_MODEL])
        w_gate = sb("w_gate", [P, K_MODEL, HIDDEN])
        w_up = sb("w_up", [P, K_MODEL, HIDDEN])
        w_down = sb("w_down", [P, H, D_MODEL])
        ident = sb("ident", [P, P])
        eps = sb("eps", [P, 1])
        marker = sb("marker", [P, 1])

        x = sb("x", [P, T, D_MODEL])
        x1 = sb("x1", [P, T, D_MODEL])
        normed_t = sb("normed_t", [P, K_MODEL, L])
        stats = sb("stats", [P, T, 6])
        mean_vars = {k: sb(f"mean_var_{k}", [P, T, 2]) for k in LAYERNORMS}
        log_vars = {k: sb(f"log_var_{k}", [P, T]) for k in LAYERNORMS}
        rstds = {k: sb(f"rstd_{k}", [P, T]) for k in LAYERNORMS}
        shifts = sb("shifts", [P, T])
        x_in = sb("x_in", [P, J, L + 2 * PAD])
        xc = sb("xc", [P, 2, J, L])
        proj = sb("proj", [PROJ + 1, 2, L])
        c_nat = sb("c_nat", [P, 2, 2, T, N_STATE])
        sp_e = sb("sp_e", [P, L])
        sp_log = sb("sp_log", [P, L])
        sp_w = sb("sp_w", [P, L])
        sp_relu = sb("sp_relu", [P, L])
        dt = sb("dt", [P, 2, J, L])
        dtx = sb("dtx", [P, 2, J, L])
        b_wide = sb("b_wide", [P, RING, L])
        drive = sb("drive", [P, RING, L])
        h = sb("h", [P, 2, J, L])
        acc = sb("acc", [P, 2, T, D_INNER])
        z = sb("z", [P, T, D_INNER])
        hidden = sb("hidden", [P, H, L])
        gated_t = hidden[:, 0:J, :]
        normed = hidden[:, J:H, :].rearrange("p i (t d) -> p (i t) d", d=D_MODEL)
        gate_i32 = acc[:, :, :, :].rearrange("p a t d -> p (a t d)")[:, 0:K_MODEL * HIDDEN].bitcast(I32)
        up_i32 = acc[:, :, :, :].rearrange("p a t d -> p (a t d)")[:, K_MODEL * HIDDEN:2 * K_MODEL * HIDDEN].bitcast(I32)
        down_i32 = hidden[:, :, :].rearrange("p a b -> p (a b)")[:, 0:H * D_MODEL].bitcast(I32)
        b_rows = nc.dram_tensor("b_rows", (2, 2, N_STATE, L), F32, kind="Internal").ap()

        w_in_loaded, w_conv_loaded, w_rest_loaded, w_int_loaded = map(sem, ("w_in_loaded", "w_conv_loaded", "w_rest_loaded", "w_int_loaded"))
        ident_zeroed, ident_made, consts_made = map(sem, ("ident_zeroed", "ident_made", "consts_made"))
        rows_made, diag_made = map(sem, ("rows_made", "diag_made"))
        a_min, a_exp, a_made, int_cast = map(sem, ("a_min", "a_exp", "a_made", "int_cast"))
        x_loaded, x1_loaded, out_stored = map(sem, ("x_loaded", "x1_loaded", "out_stored"))
        decay_made, drive_made, scan_made = map(sem, ("decay_made", "drive_made", "scan_made"))
        reset_made = sem("reset_made")
        h_t_made, acc_made = map(sem, ("h_t_made", "acc_made"))
        b_wide_loaded = [sem(f"b_wide_loaded{k}") for k in range(RING)]
        b_stored = [sem(f"b_stored{r}") for r in range(2)]
        bank_filled = sem("bank_filled")
        bank_emptied = [sem(f"bank_emptied{k}") for k in range(2)]
        correction_made, exp_made, log_made, one_plus_made = map(sem, ("correction_made", "exp_made", "log_made", "one_plus_made"))
        softplus_summed, dt_made, dtx_made = map(sem, ("softplus_summed", "dt_made", "dtx_made"))
        gated = sem("gated")
        ln = {k: {e: sem(f"ln_{k}_{e}") for e in ("stats", "mean", "log", "rstd", *(("normed",) if k in ("in", "x1") else ("shift", "added")))}
              for k in LAYERNORMS}

        BANK = lambda f: banks[:, f.bank, :]

        def emptied(eng, row, *needs, free=None):
            for k in range(2):
                uses = [f for f in (Fill(row, name, arg) for name, arg in needs) if f.bank == k]
                if free is not None and free.bank == k:
                    wait(eng, bank_emptied[k], free.emptied(after=0))
                elif uses:
                    eng.wait_ge(bank_emptied[k], max(uses, key=lambda f: f.number).emptied())

        def softplus(eng, row, name, arg, part):
            r = int(name == "dt_bwd")
            made = row.count(2 * J, J * r + arg + 1)
            if part == "sum":
                eng.wait_ge(log_made, made)
                eng.tensor_tensor(sp_log[:, :], sp_log[:, :], sp_relu[:, :], ALU.add).then_inc(softplus_summed, 1)
            elif part == "dt":
                eng.wait_ge(softplus_summed, made)
                eng.wait_ge(correction_made, made)
                wait(eng, decay_made, row.count(SLOTS, -SLOTS + SLOTS // 2 * (r + 1) - J + arg + 1))
                eng.tensor_tensor(dt[:, r, arg, :], sp_log[:, :], sp_w[:, :], ALU.subtract).then_inc(dt_made, 1)
            else:
                wait(eng, drive_made, row.count(SLOTS, -SLOTS + SLOTS // 2 * (r + 1) - J + arg + 1))
                eng.wait_ge(dt_made, made)
                eng.tensor_tensor(dtx[:, r, arg, :], dt[:, r, arg, :], xc[:, r, arg, :], ALU.mult).then_inc(dtx_made, 1)

        block = ctx.enter_context(nc.Block())

        @block.sync
        def _(sp):
            def load_x(row):
                number = row.index()
                if not row.first():
                    sp.wait_ge(bank_filled, Fill(row + -1, "x_t", K_MODEL - 1).filled())
                sp.dma_start(x[:, :, :], a["u"][bass.ds(number, 1)].rearrange("b (t p) d -> p (b t) d", p=P)).then_inc(x_loaded, 16)

            def load_x1(row):
                number = row.index()
                if row.i is None:
                    wait(sp, out_stored, row.count(32, 0))
                sp.dma_start(x1[:, :, :], a["u"][bass.ds(number, 1)].rearrange("b (t p) d -> p (b t) d", p=P)).then_inc(x1_loaded, 16)

            def load_b(row, step):
                r, n = divmod(step, N_STATE)
                if n == 0 and row.i is None:
                    sp.wait_ge(b_stored[r], row.count(16, 16))
                wait(sp, drive_made, row.count(SLOTS, J * (step - RING + 1)))
                sp.dma_start(b_wide[:, step % RING, :], b_rows[row.parity, r, n:n + 1, :].partition_broadcast(P)
                             ).then_inc(b_wide_loaded[step % RING], 16)

            sp.dma_start(x[:, :, :], a["u"][0:1].rearrange("b (t p) d -> p (b t) d", p=P)).then_inc(x_loaded, 16)
            sp.dma_start(w_in[:, :, :], a["in_proj_w"].rearrange("(k p) n -> p k n", p=P)).then_inc(w_in_loaded, 16)
            for r, d in enumerate(("fwd", "bwd")):
                sp.dma_start(w_conv[:, r, :, :], a[f"{d}_conv_w"]).then_inc(w_conv_loaded, 16)
                sp.dma_start(b_conv[:, r, :], a[f"{d}_conv_b"]).then_inc(w_conv_loaded, 16)
                sp.dma_start(w_skip[:, r, :], a[f"{d}_D"]).then_inc(w_conv_loaded, 16)
                sp.dma_start(a_neg[:, r, :, :], a[f"{d}_A_log"].rearrange("(j p) n -> p j n", p=P)).then_inc(w_conv_loaded, 16)
            for r, d in enumerate(("fwd", "bwd")):
                sp.dma_start(w_xproj[:, r, :, :], a[f"{d}_x_proj_w"].rearrange("(j p) n -> p j n", p=P)).then_inc(w_rest_loaded, 16)
                sp.dma_start(w_dt[0:DT_RANK, r, :], a[f"{d}_dt_w"]).then_inc(w_rest_loaded, 16)
                sp.dma_start(w_dt[BIAS_ROW:BIAS_ROW + 1, r, :], a[f"{d}_dt_b"].rearrange("(o n) -> o n", o=1)).then_inc(w_rest_loaded, 16)
            sp.dma_start(w_out[:, :, :], a["out_proj_w"].rearrange("(j p) n -> p j n", p=P)).then_inc(w_rest_loaded, 16)
            sp.dma_start(gate_i32.rearrange("p (k n) -> p k n", k=K_MODEL), a["w_gate"].rearrange("(k p) n -> p k n", p=P)).then_inc(w_int_loaded, 16)
            sp.dma_start(up_i32.rearrange("p (k n) -> p k n", k=K_MODEL), a["w_up"].rearrange("(k p) n -> p k n", p=P)).then_inc(w_int_loaded, 16)
            sp.dma_start(down_i32.rearrange("p (i n) -> p i n", i=H), a["w_down"].rearrange("(i p) n -> p i n", p=P)).then_inc(w_int_loaded, 16)

            def unit(row, slot):
                step, j = divmod(slot, J)
                if j == 0 and step == 0:
                    load_b(row, 0)
                    load_b(row, 1)
                    load_b(row, 2)
                if j == 0 and step + 3 < STEPS:
                    load_b(row, step + 3)

            def piece(row, name, arg, part):
                if name == "x_proj":
                    emptied(sp, row, ("x_proj", arg))
                    for k in range(RING):
                        wait(sp, b_wide_loaded[k], row.count(16 * STEPS // RING, 16 if arg else -16 * STEPS // RING))
                    sp.dma_start(b_rows[row.parity, arg], proj[DT_RANK:DT_RANK + N_STATE, arg, :]).then_inc(b_stored[arg], 16)
                if name == "gate":
                    load_x1(row)
                if name == "z" and arg == 0 and not row.last():
                    load_x(row + 1)
                if name == "down_proj":
                    number = row.index()
                    sp.wait_ge(ln["ffn"]["added"], row.count(2, arg + 1))
                    sp.dma_start(out[bass.ds(number, 1), arg * 2 * P:(arg + 1) * 2 * P, :].rearrange("b (t p) d -> p (b t) d", p=P),
                                 x1[:, 2 * arg:2 * arg + 2, :]).then_inc(out_stored, 16)

            walk(sp, "sp", unit, piece, lambda row: None)
            sp.wait_ge(out_stored, 32 * BATCH)

        @block.gpsimd
        def _(pool):
            pool.memset(ident[:, :], 0.0).then_inc(ident_zeroed, 1)
            pool.wait_ge(ident_zeroed, 1)
            pool.affine_select(out=ident[:, :], in_=ident[:, :], compare_op=ALU.not_equal, fill=1.0, base=0,
                               pattern=[[-1, P]], channel_multiplier=1).then_inc(ident_made, 1)
            pool.memset(eps[:, :], LN_EPS)
            pool.memset(x_in[:, :, 0:PAD], 0.0)
            pool.memset(x_in[:, :, L + PAD:L + 2 * PAD], 0.0).then_inc(consts_made, 1)

            def unit(row, slot):
                if slot % 2:
                    return
                step, j = divmod(slot, J)
                r = step // N_STATE
                if slot == SLOTS - (RING - 1) * J - 2 and not row.last():
                    pool.wait_ge(b_stored[0], (row + 1).count(16, 16))
                    wait(pool, out_stored, row.count(32, 0))
                if slot == SLOTS // 2 - (RING - 1) * J - 2:
                    pool.wait_ge(b_stored[1], row.count(16, 16))
                if j == 0:
                    pool.wait_ge(b_wide_loaded[step % RING], row.count(16 * STEPS // RING, 16 * (step // RING + 1)))
                if step % N_STATE == 0:
                    pool.wait_ge(dtx_made, row.count(2 * J, J * r + j + 2))
                wait(pool, scan_made, row.count(SLOTS, slot + 2 - RING))
                at = slot % RING
                pool.tensor_tensor(drive[:, at:at + 2, :], dtx[:, r, j:j + 2, :],
                                   b_wide[:, step % RING, :].unsqueeze(1).broadcast_to([P, 2, L]), ALU.mult).then_inc(drive_made, 2)

            def piece(row, name, arg, part):
                if name in ("dt_fwd", "dt_bwd") and not (row.first() and name == "dt_fwd"):
                    softplus(pool, row, name, arg, part)

            walk(pool, "pool", unit, piece, lambda row: None)

        @block.scalar
        def _(act):
            act.wait_ge(consts_made, 1)
            act.preload_act_table_set("natural_log_exp_and_others")

            table = ["exp"]

            def use_table(which):
                if which == "exp" and table[0] != "exp":
                    act.preload_act_table_set("natural_log_exp_and_others")
                table[0] = which

            def unit(row, slot):
                use_table("exp")
                step, j = divmod(slot, J)
                r, n = divmod(step, N_STATE)
                if n == 0:
                    act.wait_ge(dt_made, row.count(2 * J, J * r + j + 1))
                if slot == 0 and row.i is None and row.number == 0:
                    act.wait_ge(a_made, 1)
                wait(act, scan_made, row.count(SLOTS, slot + 1 - RING + (slot + 1) % 2))
                lo = 1 - r
                act.activation(decay[:, slot % RING, lo:lo + L - 1], dt[:, r, j, lo:lo + L - 1], ACT.Exp,
                               scale=a_neg[:, r, j, n:n + 1]).then_inc(decay_made, 1)

            def read_bank(row, name, arg):
                f = Fill(row, name, arg)
                act.wait_ge(bank_filled, f.filled())
                return f, bank_emptied[f.bank]

            def rstd_of(kind, count, tiles):
                use_table("exp")
                act.wait_ge(ln[kind]["mean"], count)
                act.activation(log_vars[kind][:, tiles], mean_vars[kind][:, tiles, 1], ACT.Ln, bias=eps[:, 0:1]).then_inc(ln[kind]["log"], 1)
                act.wait_ge(ln[kind]["log"], count)
                act.activation(rstds[kind][:, tiles], log_vars[kind][:, tiles], ACT.Exp, scale=-0.5).then_inc(ln[kind]["rstd"], 1)

            def piece(row, name, arg, part):
                if name in ("norm_in", "norm_x1"):
                    rstd_of(name[5:], row.count(1, 1), slice(0, T))
                elif name in ("out_proj", "down_proj"):
                    rstd_of("attn" if name == "out_proj" else "ffn", row.count(2, arg + 1), slice(2 * arg, 2 * arg + 2))
                elif name in ("x_t", "x1_t"):
                    if name == "x_t" and arg == 0 and row.first():
                        act.wait_ge(a_min, 1)
                        act.activation(a_neg[:, :, :, :], a_neg[:, :, :, :], ACT.Exp).then_inc(a_exp, 1)
                    f, done = read_bank(row, name, arg)
                    act.activation(normed_t[:, arg, :], BANK(f), ACT.Copy).then_inc(done, 1)
                elif name == "in_proj":
                    f, done = read_bank(row, name, arg)
                    act.activation(x_in[:, arg, PAD:PAD + L], BANK(f), ACT.Copy).then_inc(done, 1)
                elif name in ("conv_fwd", "conv_bwd"):
                    r = int(name == "conv_bwd")
                    use_table("silu")
                    wait(act, dtx_made, row.count(2 * J, -J + J * r))
                    f, done = read_bank(row, name, arg)
                    act.activation(xc[:, r, arg, :], BANK(f), ACT.Silu, bias=b_conv[:, r, arg:arg + 1]).then_inc(done, 1)
                elif name == "x_proj":
                    wait(act, b_stored[arg], row.count(16, 0))
                    f, done = read_bank(row, name, arg)
                    act.activation(proj[0:PROJ, arg, :], banks[0:PROJ, f.bank, :], ACT.Copy).then_inc(done, 1)
                elif name == "c_t":
                    wait(act, acc_made, row.count(SLOTS, 1 if arg else -SLOTS))
                    f, done = read_bank(row, name, arg)
                    act.activation(c_nat[:, row.parity, arg, :, :],
                                   banks[:, f.bank, 0:T * PROJ].rearrange("p (t c) -> p t c", t=T)[:, :, DT_RANK + N_STATE:PROJ],
                                   ACT.Copy).then_inc(done, 1)
                elif name == "d_term" and not row.first():
                    f, done = read_bank(row, name, arg)
                    act.activation(acc[:, row.parity, arg, :], BANK(f), ACT.Copy).then_inc(done, 1)
                elif name in ("dt_fwd", "dt_bwd"):
                    r = int(name == "dt_bwd")
                    made = row.count(2 * J, J * r + arg + 1)
                    use_table("exp")
                    wait(act, dt_made, row.count(2 * J, J * r + arg))
                    f, done = read_bank(row, name, arg)
                    act.activation(sp_relu[:, :], BANK(f), ACT.Relu)
                    act.activation(sp_e[:, :], BANK(f), ACT.Abs).then_inc(done, 1)
                    act.wait_ge(done, f.emptied())
                    act.activation(sp_e[:, :], sp_e[:, :], ACT.Exp, scale=-1.0).then_inc(exp_made, 1)
                    act.wait_ge(exp_made, made)
                    act.activation(sp_w[:, :], sp_e[:, :], ACT.Copy, bias=1.0).then_inc(one_plus_made, 1)
                    act.activation(sp_log[:, :], sp_e[:, :], ACT.Ln, bias=1.0).then_inc(log_made, 1)
                elif name == "z":
                    wait(act, gated, row.count(T, 0))
                    use_table("silu")
                    f, done = read_bank(row, name, arg)
                    act.activation(z[:, arg, :], BANK(f), ACT.Silu).then_inc(done, 1)
                elif name == "gated_t":
                    f, done = read_bank(row, name, arg)
                    act.activation(gated_t[:, arg, :], BANK(f), ACT.Copy).then_inc(done, 1)
                elif name == "gate_proj":
                    use_table("silu")
                    f, done = read_bank(row, name, arg)
                    act.activation(hidden[:, arg, :], BANK(f), ACT.Silu, scale=SCALE).then_inc(done, 1)

            walk(act, "act", unit, piece, lambda row: None)

        @block.tensor
        def _(pe):
            def transpose_step(row, step, t):
                number = J * step + t
                pe.wait_ge(scan_made, row.count(SLOTS, J * step + J))
                wait(pe, acc_made, row.count(SLOTS, number + 1 - 2))
                for j in range(J):
                    last = pe.transpose(h_t[:, number % 2, j * P:(j + 1) * P], h[:, step % 2, j, t * P:(t + 1) * P], ident[:, :])
                last.then_inc(h_t_made, 1)

            def unit(row, slot):
                step, j = divmod(slot, J)
                if step:
                    transpose_step(row, step - 1, j)
                elif not row.first():
                    transpose_step(row + -1, STEPS - 1, j)

            def drain(row):
                for t in range(T):
                    transpose_step(row, STEPS - 1, t)

            pe.wait_ge(ident_made, 1)
            pe.wait_ge(consts_made, 1)
            pe.wait_ge(rows_made, 1)
            pe.wait_ge(w_in_loaded, 16)

            def piece(row, name, arg, chunk):
                if name not in WORK:
                    return
                chunks = WORK[name][1]
                f = Fill(row, name, arg)
                if chunk == 0:
                    emptied(pe, row, *needs(name, arg), free=f)
                    if row.first() and name == "conv_fwd":
                        pe.wait_ge(diag_made, 1)
                    if row.first() and name == "x_proj":
                        pe.wait_ge(w_rest_loaded, 16 * 7)

                def products(pairs, into=None, span=None):
                    into = BANK(f) if into is None else into
                    lo, hi = span or (0, len(pairs))
                    for k in range(lo, hi):
                        last = pe.matmul(into, *pairs[k], start=(k == 0), stop=(k == len(pairs) - 1))
                    return last

                def share(n):
                    return chunk * n // chunks, (chunk + 1) * n // chunks

                if name in ("x_t", "x1_t"):
                    pe.wait_ge(ln["in" if name == "x_t" else "x1"]["normed"], row.count(1, 1))
                    source = x if name == "x_t" else normed
                    for t in range(T):
                        last = pe.transpose(banks[:, f.bank, t * P:(t + 1) * P], source[:, t, arg * P:(arg + 1) * P], ident[:, :])
                elif name == "in_proj":
                    last = products([(w_in[:, k, arg * P:(arg + 1) * P], normed_t[:, k, :]) for k in range(K_MODEL)], span=share(K_MODEL))
                elif name in ("conv_fwd", "conv_bwd"):
                    taps = x_in[:, arg, :]
                    last = products([(conv_diag[:, 0, arg, tap, :], taps[:, tap:tap + L]) if name == "conv_fwd" else
                                     (conv_diag[:, 1, arg, tap, :], taps[:, 2 * PAD - tap:2 * PAD - tap + L])
                                     for tap in range(D_CONV)], span=share(D_CONV))
                elif name == "x_proj":
                    last = products([(w_xproj[:, arg, j, :], xc[:, arg, j, :]) for j in range(J)], banks[0:PROJ, f.bank, :], share(J))
                elif name == "c_t":
                    for t in range(T):
                        last = pe.transpose(banks[:, f.bank, t * PROJ:(t + 1) * PROJ], proj[0:PROJ, arg, t * P:(t + 1) * P], ident[0:PROJ, 0:PROJ])
                elif name in ("dt_fwd", "dt_bwd"):
                    r = int(name == "dt_bwd")
                    last = products([(w_dt[:, r, arg * P:(arg + 1) * P], proj[:, r, :])])
                elif name == "d_term":
                    for j in range(*share(J)):
                        last = products([(xc[:, r, j, arg * P:(arg + 1) * P], skip_diag[:, r, j, :]) for r in range(2)],
                                        banks[:, f.bank, j * P:(j + 1) * P])
                elif name == "z":
                    last = products([(normed_t[:, k, arg * P:(arg + 1) * P], w_in[:, k, D_INNER:2 * D_INNER]) for k in range(K_MODEL)], span=share(K_MODEL))
                elif name == "gated_t":
                    pe.wait_ge(gated, row.count(T, T))
                    for t in range(T):
                        last = pe.transpose(banks[:, f.bank, t * P:(t + 1) * P], acc[:, row.parity, t, arg * P:(arg + 1) * P], ident[:, :])
                elif name in ("gate_proj", "up_proj"):
                    w = w_gate if name == "gate_proj" else w_up
                    last = products([(w[:, k, arg * P:(arg + 1) * P], normed_t[:, k, :]) for k in range(K_MODEL)], span=share(K_MODEL))
                elif name in ("out_proj", "down_proj"):
                    source, w, n = (gated_t, w_out, J) if name == "out_proj" else (hidden, w_down, H)
                    lo, hi = share(2 * n)
                    for k in range(2):
                        t, span = 2 * arg + k, (max(lo - k * n, 0), min(hi - k * n, n))
                        if span[0] < span[1]:
                            last = products([(source[:, i, t * P:(t + 1) * P], w[:, i, :]) for i in range(n)],
                                            banks[:, f.bank, k * D_MODEL:(k + 1) * D_MODEL], span)
                if chunk == chunks - 1:
                    last.then_inc(bank_filled, 1)

            walk(pe, "pe", unit, piece, drain)

        @block.vector
        def _(dve):
            dve.memset(proj[BIAS_ROW:BIAS_ROW + 1, :, :], 1.0)
            dve.memset(w_dt[DT_RANK:PROJ, :, :], 0.0).then_inc(rows_made, 1)

            def weights():
                dve.wait_ge(ident_made, 1)
                dve.wait_ge(w_conv_loaded, 16 * 8)
                dve.tensor_scalar(a_neg[:, :, :, :], a_neg[:, :, :, :], A_LOG_MAX, None, ALU.min).then_inc(a_min, 1)
                for j in range(J):
                    for r in range(2):
                        for tap in range(D_CONV):
                            dve.tensor_scalar(conv_diag[:, r, j, tap, :], ident[:, :], w_conv[:, r, j, tap:tap + 1], None, ALU.mult)
                        last = dve.tensor_scalar(skip_diag[:, r, j, :], ident[:, :], w_skip[:, r, j:j + 1], None, ALU.mult)
                last.then_inc(diag_made, 1)
                dve.wait_ge(a_exp, 1)
                dve.tensor_scalar(a_neg[:, :, :, :], a_neg[:, :, :, :], -1.0, None, ALU.mult).then_inc(a_made, 1)
                dve.wait_ge(w_int_loaded, 16 * 3)
                flat = lambda w: w[:, :, :].rearrange("p a b -> p (a b)")
                dve.tensor_copy(flat(w_gate), gate_i32)
                dve.tensor_copy(flat(w_up), up_i32)
                dve.tensor_copy(flat(w_down), down_i32).then_inc(int_cast, 1)

            def scan(row, slot):
                step, j = divmod(slot, J)
                r, n = divmod(step, N_STATE)
                bank = slot % RING
                dve.wait_ge(decay_made, row.count(SLOTS, slot + 2))
                if n == 0:
                    first = 0 if r == 0 else L - 1
                    dve.memset(decay[:, bank:bank + 2, first:first + 1], 0.0).then_inc(reset_made, 1)
                    dve.wait_ge(reset_made, row.count(J, (J * r + j) // 2 + 1))
                dve.wait_ge(drive_made, row.count(SLOTS, slot + 2))
                wait(dve, h_t_made, row.count(SLOTS, J * (step - 1)))

                def pair(buffer, at):
                    flat = buffer[:, at:at + 2, :].rearrange("p j t -> p (j t)")
                    return flat if r == 0 else flat[:, ::-1]

                dve.tensor_tensor_scan(pair(h[:, step % 2], j), pair(decay, bank), pair(drive, bank), 0.0,
                                       ALU.mult, ALU.add).then_inc(scan_made, 2)

            first_row_sums = [0]

            def accumulate(row, step, t):
                r, n = divmod(step, N_STATE)
                number = J * step + t
                if row.first():
                    first_row_sums[0] = number + 1
                    if number == 0:
                        dve.wait_ge(int_cast, 1)
                if n == 0:
                    emptied(dve, row, ("c_t", r), *([("d_term", t)] if step == 0 and not row.first() else []))
                dve.wait_ge(h_t_made, row.count(SLOTS, number + 1))
                summed, c = acc[:, row.parity, t, :], c_nat[:, row.parity, r, t, n:n + 1]
                if step == 0 and row.first():
                    dve.tensor_scalar(summed, h_t[:, number % 2, :], c, None, ALU.mult).then_inc(acc_made, 1)
                    return
                if step:
                    dve.wait_ge(acc_made, row.count(SLOTS, number + 1 - T))
                dve.scalar_tensor_tensor(out=summed, in0=h_t[:, number % 2, :], scalar=c, in1=summed, op0=ALU.mult, op1=ALU.add
                                         ).then_inc(acc_made, 1)

            def unit(row, slot):
                if slot % 2 == 0:
                    scan(row, slot)
                step, t = divmod(slot - J, J)
                if step >= 0:
                    accumulate(row, step, t)
                elif not row.first():
                    accumulate(row + -1, STEPS + step, t)

            def drain(row):
                for number in range(SLOTS - J, SLOTS):
                    accumulate(row, *divmod(number, J))

            def moments(kind, count, src, tiles):
                for k, t in enumerate(tiles):
                    last = dve.bn_stats(stats[:, t, :], src(k))
                last.then_inc(ln[kind]["stats"], 1)
                dve.wait_ge(ln[kind]["stats"], count)
                dve.memset(marker[:, :], 0.0)
                for t in tiles:
                    last = dve.bn_aggr(mean_vars[kind][:, t, :], stats[:, t, :])
                last.then_inc(ln[kind]["mean"], 1)

            def normalise(kind, count, src, into):
                dve.wait_ge(ln[kind]["rstd"], count)
                for t in range(T):
                    last = dve.tensor_scalar(into[:, t, :], src[:, t, :], mean_vars[kind][:, t, 0:1], rstds[kind][:, t:t + 1], ALU.subtract, ALU.mult)
                return last

            def piece(row, name, arg, part):
                if name == "norm_in":
                    if part == "stats":
                        dve.wait_ge(x_loaded, row.count(16, 16))
                        wait(dve, ln["x1"]["mean"], row.count(1, -1))
                        moments("in", row.count(1, 1), lambda t: x[:, t, :], range(T))
                        return
                    normalise("in", row.count(1, 1), x, x).then_inc(ln["in"]["normed"], 1)
                    if row.i is None and row.number == 0:
                        weights()
                elif name == "d_term" and row.first():
                    f = Fill(row, name, arg)
                    dve.wait_ge(bank_filled, f.filled())
                    dve.wait_ge(acc_made, first_row_sums[0])
                    dve.tensor_tensor(acc[:, 0, arg, :], acc[:, 0, arg, :], BANK(f), ALU.add).then_inc(bank_emptied[f.bank], 1)
                    dve.wait_ge(bank_emptied[f.bank], f.emptied())
                elif name in ("dt_fwd", "dt_bwd"):
                    r = int(name == "dt_bwd")
                    made = row.count(2 * J, J * r + arg + 1)
                    dve.wait_ge(one_plus_made, made)
                    dve.scalar_tensor_tensor(out=sp_w[:, :], in0=sp_w[:, :], scalar=1.0, in1=sp_e[:, :], op0=ALU.subtract, op1=ALU.subtract
                                             ).then_inc(correction_made, 1)
                    if row.first() and r == 0:
                        for step in ("sum", "dt", ""):
                            softplus(dve, row, name, arg, step)
                elif name == "gate":
                    emptied(dve, row, *[("z", t) for t in range(T)])
                    dve.wait_ge(acc_made, row.count(SLOTS, SLOTS))
                    for t in range(T):
                        dve.tensor_tensor(acc[:, row.parity, t, :], acc[:, row.parity, t, :], z[:, t, :], ALU.mult).then_inc(gated, 1)
                elif name in ("out_proj", "down_proj"):
                    kind = "attn" if name == "out_proj" else "ffn"
                    count = row.count(2, arg + 1)
                    tiles = range(2 * arg, 2 * arg + 2)
                    f = Fill(row, name, arg)
                    rows = lambda k: banks[:, f.bank, k * D_MODEL:(k + 1) * D_MODEL]
                    if part == "stats":
                        dve.wait_ge(bank_filled, f.filled())
                        moments(kind, count, rows, tiles)
                        return
                    two = slice(2 * arg, 2 * arg + 2)
                    dve.wait_ge(ln[kind]["rstd"], count)
                    dve.tensor_tensor(shifts[:, two], mean_vars[kind][:, two, 0], rstds[kind][:, two], ALU.mult).then_inc(ln[kind]["shift"], 1)
                    if name == "out_proj":
                        dve.wait_ge(x1_loaded, row.count(16, 16))
                    for k, t in enumerate(tiles):
                        last = dve.scalar_tensor_tensor(out=x1[:, t, :], in0=rows(k), scalar=rstds[kind][:, t:t + 1], in1=x1[:, t, :],
                                                        op0=ALU.mult, op1=ALU.add)
                    last.then_inc(bank_emptied[f.bank], 1)
                    dve.wait_ge(ln[kind]["shift"], count)
                    dve.wait_ge(bank_emptied[f.bank], f.emptied())
                    for t in tiles:
                        last = dve.tensor_scalar(x1[:, t, :], x1[:, t, :], shifts[:, t:t + 1], None, ALU.subtract)
                    last.then_inc(ln[kind]["added"], 1)
                elif name == "norm_x1":
                    if part == "stats":
                        dve.wait_ge(ln["attn"]["added"], row.count(2, 2))
                        moments("x1", row.count(1, 1), lambda t: x1[:, t, :], range(T))
                        return
                    normalise("x1", row.count(1, 1), x1, normed).then_inc(ln["x1"]["normed"], 1)
                elif name == "up_proj":
                    f = Fill(row, name, arg)
                    dve.wait_ge(bank_filled, f.filled())
                    emptied(dve, row, ("gate_proj", arg))
                    dve.scalar_tensor_tensor(out=hidden[:, arg, :], in0=BANK(f), scalar=SCALE * SCALE, in1=hidden[:, arg, :],
                                             op0=ALU.mult, op1=ALU.mult).then_inc(bank_emptied[f.bank], 1)

            walk(dve, "dve", unit, piece, drain)


_NAMES = {
    "u": "L0_attn_u", "in_proj_w": "L0_attn_in_proj_w", "out_proj_w": "L0_attn_out_proj_w",
    "fwd_conv_w": "L0_attn_fwd_conv_w", "fwd_conv_b": "L0_attn_fwd_conv_b", "fwd_x_proj_w": "L0_attn_fwd_x_proj_w",
    "fwd_dt_w": "L0_attn_fwd_dt_w", "fwd_dt_b": "L0_attn_fwd_dt_b", "fwd_A_log": "L0_attn_fwd_A_log", "fwd_D": "L0_attn_fwd_D",
    "bwd_conv_w": "L0_attn_bwd_conv_w", "bwd_conv_b": "L0_attn_bwd_conv_b", "bwd_x_proj_w": "L0_attn_bwd_x_proj_w",
    "bwd_dt_w": "L0_attn_bwd_dt_w", "bwd_dt_b": "L0_attn_bwd_dt_b", "bwd_A_log": "L0_attn_bwd_A_log", "bwd_D": "L0_attn_bwd_D",
    "w_gate": "L0_ffn_w_gate", "w_up": "L0_ffn_w_up", "w_down": "L0_ffn_w_down",
}
_TRANSPOSED = ("in_proj_w", "out_proj_w", "fwd_x_proj_w", "bwd_x_proj_w", "fwd_dt_w", "bwd_dt_w", "w_gate", "w_up", "w_down")
_CHANNELS = ("fwd_conv_w", "fwd_conv_b", "fwd_D", "bwd_conv_w", "bwd_conv_b", "bwd_D")


def kernel(**inputs):
    import numpy as _np
    import concourse.bacc as _bacc
    from concourse import mybir as _mybir
    from concourse.bass_utils import run_bass_kernel_spmd as _run

    nc = _bacc.Bacc("TRN2", target_bir_lowering=False, num_devices=1)
    arrays, args = {}, {}
    for name, given in _NAMES.items():
        v = _np.asarray(inputs[given])
        if name in _TRANSPOSED:
            v = v.T
        elif name in _CHANNELS:
            v = _np.moveaxis(v.reshape(J, P, *[n for n in v.shape[1:] if n > 1]), 0, 1)
        v = _np.ascontiguousarray(v)
        arrays[f"in_{name}"] = v
        args[name] = nc.dram_tensor(f"in_{name}", v.shape, _mybir.dt.from_np(v.dtype), kind="ExternalInput").ap()
    out = nc.dram_tensor("out", (BATCH, L, D_MODEL), _mybir.dt.float32, kind="ExternalOutput").ap()
    build(nc, args, out)
    r = _run(nc, [arrays], core_ids=[0])
    return r.results[0]["out"]
```
